# Optimizing a Trainium2 kernel written in Bass

```python
import numpy as np
import jax
import jax.numpy as jnp

def _softmax(x, axis=-1):
    return jax.nn.softmax(x, axis=axis)

def _gelu(x):
    return jax.nn.gelu(x, approximate=True)

def _silu(x):
    return jax.nn.silu(x)

def _sigmoid(x):
    return jax.nn.sigmoid(x)

def _layernorm(x, axis=-1, eps=1e-05):
    m = jnp.mean(x, axis=axis, keepdims=True)
    v = jnp.var(x, axis=axis, keepdims=True)
    return (x - m) / jnp.sqrt(v + eps)

def _scatter_add(tgt, idx, src, axis=0):
    return tgt.at[idx].add(src)

def _segment_sum(src, seg, n):
    return jax.ops.segment_sum(src, seg, n)
kernel_name = 'mk_macaron_d2_jaxref_r8_7b09b0'

def setup_inputs(seed: int=0):
    np.random.seed(seed)
    _w = jnp.asarray

    def _L0_attn_setup():
        import jax, jax.numpy as jnp
        import numpy as np
        CHUNK = 32
        ROPE_BASE = 10000.0
        EPS = 1e-06

        def _rmsnorm(x, scale):
            xf = x.astype(jnp.float32)
            rms = jax.lax.rsqrt(jnp.mean(xf * xf, axis=-1, keepdims=True) + EPS)
            out = scale.astype(jnp.float32) * (xf * rms)
            return jnp.clip(out, -60000.0, 60000.0).astype(x.dtype)

        def _rope(v, N, d_head, dtype):
            half = d_head // 2
            inv_freq = 1.0 / ROPE_BASE ** (jnp.arange(0, d_head, 2, dtype=jnp.float32) / d_head)
            freqs = jnp.arange(N, dtype=jnp.float32)[:, None] * inv_freq[None, :]
            cos = jnp.cos(freqs).astype(dtype)[None, :, None, :]
            sin = jnp.sin(freqs).astype(dtype)[None, :, None, :]
            v1, v2 = (v[..., :half], v[..., half:])
            return jnp.concatenate([v1 * cos - v2 * sin, v1 * sin + v2 * cos], axis=-1)
        key = jax.random.key(seed)
        ks = jax.random.split(key, 8)
        B, N, D, H, K = (4, 1024, 128, 16, 4)
        x = jax.random.normal(ks[0], (B, N, D), dtype=jnp.float32)
        norm_scale = jnp.ones((D,), dtype=jnp.float32)
        conv_w = jax.random.normal(ks[1], (D, 1, K), dtype=jnp.float32) * 0.2
        conv_b = jax.random.normal(ks[2], (D,), dtype=jnp.float32) * 0.02
        in_proj_w = jax.random.normal(ks[3], (D, 3 * D), dtype=jnp.float32) * 0.02
        dt_bias = jax.random.normal(ks[4], (D,), dtype=jnp.float32) * 0.5
        head_mix = jnp.eye(H, dtype=jnp.float32) + 0.02 * jax.random.normal(ks[5], (H, H), dtype=jnp.float32)
        out_proj_w = jax.random.normal(ks[6], (D, D), dtype=jnp.float32) * 0.02
        return {'x': x, 'norm_scale': norm_scale, 'conv_w': conv_w, 'conv_b': conv_b, 'in_proj_w': in_proj_w, 'dt_bias': dt_bias, 'head_mix': head_mix, 'out_proj_w': out_proj_w}
    _L0_attn_in = _L0_attn_setup()

    def _L0_ffn_setup():
        import jax, jax.numpy as jnp
        import numpy as np
        E = 8
        JITTER = 0.01

        def _sparse_mixer_routing(logits):
            top_vals, top_idx = jax.lax.top_k(logits, 2)
            eidx = jnp.arange(logits.shape[-1])

            def _multiplier(thr, base_logits, idx):
                factor = jnp.maximum(jnp.abs(logits), thr)
                mask = (thr - logits) / factor > 2.0 * JITTER
                probs = jax.nn.softmax(jnp.where(mask, -jnp.inf, base_logits), axis=-1)
                return jnp.take_along_axis(probs, idx, axis=-1)
            mult1 = _multiplier(top_vals[:, :1], logits, top_idx[:, :1])
            scat = jnp.where(eidx[None, :] == top_idx[:, :1], -jnp.inf, logits)
            mult2 = _multiplier(top_vals[:, 1:2], scat, top_idx[:, 1:2])
            return (jnp.concatenate([mult1, mult2], axis=-1), top_idx)
        key = jax.random.key(seed)
        ks = jax.random.split(key, 5)
        H, F = (128, 512)
        scale = 0.02
        return {'hidden_states': jax.random.normal(ks[0], (1, 256, H), jnp.float32), 'gate_w': jax.random.normal(ks[1], (H, E), jnp.float32) * scale, 'w1': jax.random.normal(ks[2], (E, H, F), jnp.float32) * scale, 'w2': jax.random.normal(ks[3], (E, F, H), jnp.float32) * scale, 'w3': jax.random.normal(ks[4], (E, H, F), jnp.float32) * scale}
    _L0_ffn_in = _L0_ffn_setup()

    def _L1_attn_setup():
        import jax, jax.numpy as jnp
        import numpy as np
        NEG_INF = -1e+30
        key = jax.random.key(seed)
        k1, k2, k3 = jax.random.split(key, 3)
        B, S, D, H = (4, 256, 128, 16)
        dk = D // H
        x = jax.random.normal(k1, (B, S, D), dtype=jnp.float32)
        bound = 1.0 / np.sqrt(D)
        W_qkv = jax.random.uniform(k2, (3, H, dk, D), dtype=jnp.float32, minval=-bound, maxval=bound)
        W_o = jax.random.uniform(k3, (D, H * dk), dtype=jnp.float32, minval=-bound, maxval=bound)
        return {'x': x, 'W_qkv': W_qkv, 'W_o': W_o}
    _L1_attn_in = _L1_attn_setup()

    def _L1_ffn_setup():
        import jax, jax.numpy as jnp
        import numpy as np
        DIM = 128

        def _reference_tuple_inner(x, W_r, W_k, W_v, mu_r, mu_k):
            B, T, C = x.shape
            x_prev = jnp.concatenate([jnp.zeros((B, 1, C), x.dtype), x[:, :-1, :]], axis=1)
            xr = mu_r * x + (1.0 - mu_r) * x_prev
            xk = mu_k * x + (1.0 - mu_k) * x_prev
            r = jax.nn.sigmoid(jnp.einsum('btc,dc->btd', xr, W_r))
            k = jnp.einsum('btc,dc->btd', xk, W_k)
            k_act = jnp.square(jax.nn.relu(k))
            out = r * jnp.einsum('btc,dc->btd', k_act, W_v)
            new_state = x[:, -1, :]
            return (out, new_state)
        key = jax.random.key(seed)
        ks = jax.random.split(key, 6)
        B, T, C = (8, 256, DIM)
        x = jax.random.normal(ks[0], (B, T, C), dtype=jnp.float32)
        s = 1.0 / np.sqrt(C)
        W_r = jax.random.uniform(ks[1], (C, C), jnp.float32, -s, s)
        W_k = jax.random.uniform(ks[2], (C, C), jnp.float32, -s, s)
        W_v = jax.random.uniform(ks[3], (C, C), jnp.float32, -s, s)
        mu_r = jax.random.uniform(ks[4], (C,), jnp.float32)
        mu_k = jax.random.uniform(ks[5], (C,), jnp.float32)
        return {'x': x, 'W_r': W_r, 'W_k': W_k, 'W_v': W_v, 'mu_r': mu_r, 'mu_k': mu_k}
    _L1_ffn_in = _L1_ffn_setup()
    _d = {'L0_attn_x': _L0_attn_in['x'], 'L0_attn_norm_scale': _L0_attn_in['norm_scale'], 'L0_attn_conv_w': _L0_attn_in['conv_w'], 'L0_attn_conv_b': _L0_attn_in['conv_b'], 'L0_attn_in_proj_w': _L0_attn_in['in_proj_w'], 'L0_attn_dt_bias': _L0_attn_in['dt_bias'], 'L0_attn_head_mix': _L0_attn_in['head_mix'], 'L0_attn_out_proj_w': _L0_attn_in['out_proj_w'], 'L0_ffn_gate_w': _L0_ffn_in['gate_w'], 'L0_ffn_w1': _L0_ffn_in['w1'], 'L0_ffn_w2': _L0_ffn_in['w2'], 'L0_ffn_w3': _L0_ffn_in['w3'], 'L1_attn_W_qkv': _L1_attn_in['W_qkv'], 'L1_attn_W_o': _L1_attn_in['W_o'], 'L1_ffn_W_r': _L1_ffn_in['W_r'], 'L1_ffn_W_k': _L1_ffn_in['W_k'], 'L1_ffn_W_v': _L1_ffn_in['W_v'], 'L1_ffn_mu_r': _L1_ffn_in['mu_r'], 'L1_ffn_mu_k': _L1_ffn_in['mu_k']}
    _x0 = _d['L0_attn_x']
    _d['L0_attn_x'] = jax.random.normal(jax.random.fold_in(jax.random.key(seed), 1), (8, 512, 128), dtype=_x0.dtype)
    del _x0
    return _d

def reference(L0_attn_x, L0_attn_norm_scale, L0_attn_conv_w, L0_attn_conv_b, L0_attn_in_proj_w, L0_attn_dt_bias, L0_attn_head_mix, L0_attn_out_proj_w, L0_ffn_gate_w, L0_ffn_w1, L0_ffn_w2, L0_ffn_w3, L1_attn_W_qkv, L1_attn_W_o, L1_ffn_W_r, L1_ffn_W_k, L1_ffn_W_v, L1_ffn_mu_r, L1_ffn_mu_k):

    def _L0_attn_ref(x, norm_scale, conv_w, conv_b, in_proj_w, dt_bias, head_mix, out_proj_w):
        import jax, jax.numpy as jnp
        import numpy as np
        CHUNK = 32
        ROPE_BASE = 10000.0
        EPS = 1e-06

        def _rmsnorm(x, scale):
            xf = x.astype(jnp.float32)
            rms = jax.lax.rsqrt(jnp.mean(xf * xf, axis=-1, keepdims=True) + EPS)
            out = scale.astype(jnp.float32) * (xf * rms)
            return jnp.clip(out, -60000.0, 60000.0).astype(x.dtype)

        def _rope(v, N, d_head, dtype):
            half = d_head // 2
            inv_freq = 1.0 / ROPE_BASE ** (jnp.arange(0, d_head, 2, dtype=jnp.float32) / d_head)
            freqs = jnp.arange(N, dtype=jnp.float32)[:, None] * inv_freq[None, :]
            cos = jnp.cos(freqs).astype(dtype)[None, :, None, :]
            sin = jnp.sin(freqs).astype(dtype)[None, :, None, :]
            v1, v2 = (v[..., :half], v[..., half:])
            return jnp.concatenate([v1 * cos - v2 * sin, v1 * sin + v2 * cos], axis=-1)
        residual = x
        B, N, D = x.shape
        H = head_mix.shape[0]
        d_head = D // H
        xn = _rmsnorm(x, norm_scale)
        K = conv_w.shape[-1]
        xc = jax.lax.conv_general_dilated(xn.transpose(0, 2, 1), conv_w, window_strides=(1,), padding=[(K - 1, 0)], feature_group_count=D, dimension_numbers=('NCH', 'OIH', 'NCH'))
        xc = (xc + conv_b[None, :, None]).transpose(0, 2, 1)
        xc = xc * jax.nn.sigmoid(xc)
        fused = xc @ in_proj_w
        dt_raw, v, gate_raw = jnp.split(fused, 3, axis=-1)
        dt = jnp.clip(jax.nn.softplus(dt_raw.astype(jnp.float32) + dt_bias.astype(jnp.float32)), 0.001, 2.0).astype(dt_raw.dtype)
        gate = jax.nn.sigmoid(gate_raw)
        log_alpha = -dt.astype(jnp.float32)
        v_rot = _rope(v.reshape(B, N, H, d_head), N, d_head, x.dtype).reshape(B, N, D)
        v_in = (v_rot * dt).astype(jnp.float32)
        pad = -N % CHUNK
        if pad:
            v_in = jnp.pad(v_in, ((0, 0), (0, pad), (0, 0)))
            log_alpha = jnp.pad(log_alpha, ((0, 0), (0, pad), (0, 0)))
        Np = N + pad
        nc = Np // CHUNK
        v_ch = v_in.reshape(B, nc, CHUNK, D)
        la_ch = log_alpha.reshape(B, nc, CHUNK, D)
        L = jnp.clip(jnp.cumsum(la_ch, axis=2), -20.0, 0.0)
        L_max = jnp.max(L, axis=2, keepdims=True)
        L_st = L - L_max
        cum_scaled = jnp.cumsum(jnp.exp(-L_st) * v_ch, axis=2)
        chunk_out = jnp.exp(L_st) * cum_scaled
        if nc > 1:
            bdecay = L[:, :, -1, :]
            bout = chunk_out[:, :, -1, :]
            cum_decay = jnp.clip(jnp.cumsum(bdecay, axis=1), -80.0, 0.0)
            stab = jnp.max(cum_decay, axis=1, keepdims=True)
            ncd = jnp.clip(cum_decay - stab, -20.0, 0.0)
            seeds = bout * jnp.exp(-ncd)
            shifted = jnp.pad(seeds[:, :-1], ((0, 0), (1, 0), (0, 0)))
            carries = jnp.cumsum(shifted, axis=1) * jnp.exp(ncd)
            final = chunk_out + carries[:, :, None, :] * jnp.exp(L)
        else:
            final = chunk_out
        final = final.astype(x.dtype).reshape(B, Np, D)[:, :N, :]
        v_mix = jnp.einsum('bnhd,hm->bnmd', final.reshape(B, N, H, d_head), head_mix)
        final = v_mix.reshape(B, N, D)
        out = final * gate @ out_proj_w
        return residual + out

    def _L0_ffn_ref(hidden_states, gate_w, w1, w2, w3):
        import jax, jax.numpy as jnp
        import numpy as np
        E = 8
        JITTER = 0.01

        def _sparse_mixer_routing(logits):
            top_vals, top_idx = jax.lax.top_k(logits, 2)
            eidx = jnp.arange(logits.shape[-1])

            def _multiplier(thr, base_logits, idx):
                factor = jnp.maximum(jnp.abs(logits), thr)
                mask = (thr - logits) / factor > 2.0 * JITTER
                probs = jax.nn.softmax(jnp.where(mask, -jnp.inf, base_logits), axis=-1)
                return jnp.take_along_axis(probs, idx, axis=-1)
            mult1 = _multiplier(top_vals[:, :1], logits, top_idx[:, :1])
            scat = jnp.where(eidx[None, :] == top_idx[:, :1], -jnp.inf, logits)
            mult2 = _multiplier(top_vals[:, 1:2], scat, top_idx[:, 1:2])
            return (jnp.concatenate([mult1, mult2], axis=-1), top_idx)
        B, S, H = hidden_states.shape
        x = hidden_states.reshape(-1, H)
        logits = x @ gate_w
        mult, sel = _sparse_mixer_routing(logits)
        w = jnp.sum(mult[:, :, None] * (sel[:, :, None] == jnp.arange(E)[None, None, :]), axis=1)
        h = jax.nn.silu(jnp.einsum('th,ehf->etf', x, w1)) * jnp.einsum('th,ehf->etf', x, w3)
        out = jnp.einsum('etf,efh,te->th', h, w2, w)
        return out.reshape(B, S, H)

    def _L1_attn_ref(x, W_qkv, W_o):
        import jax, jax.numpy as jnp
        import numpy as np
        NEG_INF = -1e+30
        B, S, M = x.shape
        _, H, dk, _ = W_qkv.shape
        qkv = jnp.einsum('bsm,qhdm->qbhsd', x, W_qkv)
        Q, K, V = (qkv[0], qkv[1], qkv[2])
        scale = 1.0 / np.sqrt(dk)
        scores = jnp.einsum('bhqd,bhkd->bhqk', Q, K)
        causal_mask = jnp.triu(jnp.ones((S, S), dtype=bool), k=1)
        scores = jnp.where(causal_mask, NEG_INF, scores) * scale
        attn = jax.nn.softmax(scores, axis=-1)
        ctx = jnp.einsum('bhqk,bhkd->bhqd', attn, V)
        concat = jnp.transpose(ctx, (0, 2, 1, 3)).reshape(B, S, H * dk)
        return jnp.einsum('sf,df->sd'.replace('s', 'bs'), concat, W_o) if False else jnp.einsum('bsf,df->bsd', concat, W_o)

    def _L1_ffn_ref(x, W_r, W_k, W_v, mu_r, mu_k):
        import jax, jax.numpy as jnp
        import numpy as np
        DIM = 128

        def _reference_tuple_inner(x, W_r, W_k, W_v, mu_r, mu_k):
            B, T, C = x.shape
            x_prev = jnp.concatenate([jnp.zeros((B, 1, C), x.dtype), x[:, :-1, :]], axis=1)
            xr = mu_r * x + (1.0 - mu_r) * x_prev
            xk = mu_k * x + (1.0 - mu_k) * x_prev
            r = jax.nn.sigmoid(jnp.einsum('btc,dc->btd', xr, W_r))
            k = jnp.einsum('btc,dc->btd', xk, W_k)
            k_act = jnp.square(jax.nn.relu(k))
            out = r * jnp.einsum('btc,dc->btd', k_act, W_v)
            new_state = x[:, -1, :]
            return (out, new_state)
        return _reference_tuple_inner(x, W_r, W_k, W_v, mu_r, mu_k)[0]
    x = L0_attn_x
    x = x + 0.5 * _L0_ffn_ref(_layernorm(x, axis=-1), L0_ffn_gate_w, L0_ffn_w1, L0_ffn_w2, L0_ffn_w3)
    x = x + _L0_attn_ref(_layernorm(x, axis=-1), L0_attn_norm_scale, L0_attn_conv_w, L0_attn_conv_b, L0_attn_in_proj_w, L0_attn_dt_bias, L0_attn_head_mix, L0_attn_out_proj_w)
    x = x + 0.5 * _L0_ffn_ref(_layernorm(x, axis=-1), L0_ffn_gate_w, L0_ffn_w1, L0_ffn_w2, L0_ffn_w3)
    x = x + 0.5 * _L1_ffn_ref(_layernorm(x, axis=-1), L1_ffn_W_r, L1_ffn_W_k, L1_ffn_W_v, L1_ffn_mu_r, L1_ffn_mu_k)
    x = x + _L1_attn_ref(_layernorm(x, axis=-1), L1_attn_W_qkv, L1_attn_W_o)
    x = x + 0.5 * _L1_ffn_ref(_layernorm(x, axis=-1), L1_ffn_W_r, L1_ffn_W_k, L1_ffn_W_v, L1_ffn_mu_r, L1_ffn_mu_k)
    return x

_drawn_inputs = setup_inputs


def setup_inputs(seed=0):
    import zlib

    import numpy as np

    out = dict(_drawn_inputs(seed))
    spreads = {'L0_attn_norm_scale': (1.0, 0.6)}
    factors = {'L0_attn_conv_w': 8.0,
     'L0_attn_conv_b': 8.0,
     'L0_attn_in_proj_w': 8.0,
     'L0_attn_dt_bias': 8.0,
     'L0_attn_head_mix': 8.0,
     'L0_attn_out_proj_w': 8.0,
     'L0_ffn_gate_w': 5.244,
     'L0_ffn_w1': 4.606,
     'L0_ffn_w2': 4.574,
     'L0_ffn_w3': 4.578,
     'L1_attn_W_qkv': 22.48,
     'L1_attn_W_o': 21.864,
     'L1_ffn_W_r': 50.184,
     'L1_ffn_mu_r': 64.0,
     'L1_ffn_W_k': 8.0,
     'L1_ffn_W_v': 8.0,
     'L1_ffn_mu_k': 8.0}
    for name, (base, spread) in spreads.items():
        noise = np.random.default_rng([zlib.crc32(name.encode()), seed]).standard_normal(out[name].shape)
        drawn = base * np.exp(spread * noise) if base else spread * noise
        out[name] = jnp.asarray(drawn.astype(out[name].dtype))
    for name, factor in factors.items():
        out[name] = (out[name] * factor).astype(out[name].dtype)
    return out
```

```python
import math
from contextlib import ExitStack

import numpy as np

import concourse.bass as bass
from concourse import mybir

F32 = mybir.dt.float32
F32R = mybir.dt.float32r
BF16 = mybir.dt.bfloat16
I32 = mybir.dt.int32
U32 = mybir.dt.uint32
ALU = mybir.AluOpType
ACT = mybir.ActivationFunctionType
AX = mybir.AxisListType
LN_EXP = "natural_log_exp_and_others"

P = 128
B, S, D = 8, 512, 128
T = B * S
TILES = T // P
TPB = S // P
E, FF = 8, 512
FC = FF // P
SLOT_TILES = (2 * T) // P + E
EPS_LN, EPS_RMS = 1e-5, 1e-6
HM = 16
DH = D // HM
KC = 4
CHUNK = 32
CHUNKS = S // CHUNK
ROPE_BASE = 10000.0
HA = 16
DK = D // HA
GH = 4
GROUPS = HA // GH
QR = P // GH
MH_ROW, ML_ROW = 3 * DK, 3 * DK + 1
NEG = -1e30

CONST = {}
_at = 0
for _name, _width in (("bias_k", 1), ("pick_q", 1), ("pick_k", 1), ("ident", P), ("before", P), ("ones", P), ("rev", TILES * E), ("newexp", E * TILES),
                      ("tile0", SLOT_TILES), ("cos", S), ("sin", S), ("newchunk", S)):
    CONST[_name] = slice(_at, _at + _width)
    _at += _width
CONST_COLS = _at


def constant_table():
    c = np.zeros((P, CONST_COLS), np.float32)
    p = np.arange(P)
    c[:, CONST["ident"]] = np.eye(P)
    c[:, CONST["before"]] = p[:, None] < p[None, :]
    c[:, CONST["ones"]] = 1.0
    c[:, CONST["rev"]] = np.tile(E - np.arange(E), TILES)
    newexp = np.ones((E, TILES))
    newexp[:, 0] = 0
    c[:, CONST["newexp"]] = newexp.ravel()
    c[:, CONST["tile0"]] = P * np.arange(SLOT_TILES)
    row = p % QR
    c[:, CONST["pick_q"]] = ((row >= 2 * DK) & (row < 3 * DK))[:, None]
    c[:, CONST["pick_k"]] = ((row >= DK) & (row < 2 * DK))[:, None]
    c[:, CONST["bias_k"]] = -1.0 * ((row == MH_ROW) | (row == ML_ROW))[:, None]
    freq = (np.float32(1.0) / np.float32(ROPE_BASE) ** (np.arange(0, DH, 2, dtype=np.float32) / np.float32(DH)))
    angle = np.arange(S, dtype=np.float32)[None, :] * freq.astype(np.float32)[(p % DH) % (DH // 2)][:, None]
    c[:, CONST["cos"]] = np.cos(angle)
    c[:, CONST["sin"]] = np.sin(angle) * np.where(p % DH < DH // 2, -1.0, 1.0)[:, None]
    c[:, CONST["newchunk"]] = (np.arange(S) % CHUNK != 0)
    return c


class Chain:

    def __init__(self, eng, sem, start=0):
        self.eng, self.sem, self.start, self.n = eng, sem, start, 0

    def link(self, ins):
        ins.then_inc(self.sem, 1)
        self.n += 1
        self.eng.wait_ge(self.sem, self.start + self.n)


def build_macaron(nc, x, consts, gate_w, w1, w3, w2, vecs, conv_diag, in_proj, head_mix, out_proj, ffn_w, w_q, w_k, w_v, w_o, masks, out):
    with ExitStack() as ctx:
        sb = lambda name, shape, dt=F32, c=ctx: c.enter_context(nc.sbuf_tensor(name, shape, dt))
        ps = lambda name, shape, dt=F32, c=ctx: c.enter_context(nc.psum_tensor(name, shape, dt))
        sem = nc.alloc_semaphore
        no_semaphores = nc.snapshot_sems()

        X = sb("X", [P, TILES, D])
        CT = sb("CT", [P, CONST_COLS])
        IDENT, BEFORE, ONES = CT[:, CONST["ident"]], CT[:, CONST["before"]], CT[:, CONST["ones"]]
        XS = nc.dram_tensor("xs_scratch", (SLOT_TILES * P, D), F32).ap()
        YS = nc.dram_tensor("ys_scratch", (SLOT_TILES * P, D), F32).ap()
        x_tok = x.rearrange("(t p) d -> p t d", p=P)
        out_tok = out.rearrange("(t p) d -> p t d", p=P)

        VEC = sb("VEC", [P, 8 + KC])
        NORM_SCALE, CONV_B, DT_BIAS, MU_R, MU_K = (VEC[:, v:v + 1] for v in range(5))

        def some_wait(eng, s, v):
            if not isinstance(v, int) or v > 0:
                eng.wait_ge(s, v)

        def over_batches(eng, body):
            body(None, 1, 0)
            body(0, 0, 1)
            body(1, 1, 2)
            with eng.Fori(1, B // 2 - 1) as i:
                for h in range(2):
                    body(i * 2 + h, h, i * 2 + h + 1)
            body(B - 2, 0, B - 1)
            body(B - 1, 1, None)

        def rsqrt(name, src, dst, c):
            Y0, LNV, A0, A1, A2 = (sb(f"{name}_r{k}", [P, TILES], F32, c) for k in range(5))
            src_ready, ln_done, guess_done, link_sem = (sem(f"{name}_{s}") for s in (
                "src_ready", "ln_done", "guess_done", "rsqrt_link"))

            def on_scalar(act):
                act.wait_ge(src_ready, 1)
                nc.scalar.activation(LNV[:], src, ACT.Ln).then_inc(ln_done, 1)
                act.wait_ge(ln_done, 1)
                nc.scalar.activation(Y0[:], LNV[:], ACT.Exp, scale=-0.5).then_inc(guess_done, 1)

            def on_vector(dve):
                dve.wait_ge(guess_done, 1)
                ch = Chain(dve, link_sem)
                ch.link(nc.vector.tensor_tensor(A0[:], Y0[:], Y0[:], ALU.mult))
                ch.link(nc.vector.tensor_tensor(A1[:], A0[:], src, ALU.mult))
                ch.link(nc.vector.tensor_scalar(A2[:], A1[:], -0.5, 1.5, ALU.mult, ALU.add))
                ch.link(nc.vector.tensor_tensor(dst, Y0[:], A2[:], ALU.mult))

            return src_ready, on_vector, on_scalar

        def layernorm(name, c):
            ST = sb(name + "_ST", [P, TILES, 6], F32, c)
            MEAN, RSTD, VAR, VARE, A0, A1 = (sb(f"{name}_t{k}", [P, TILES], F32, c) for k in range(6))
            stats_done, link_sem = sem(name + "_stats_done"), sem(name + "_link")
            var_ready, root_vector, root_scalar = rsqrt(name, VARE[:], RSTD[:], c)

            def on_vector(dve):
                with dve.Fori(0, B) as b:
                    for u in range(TPB):
                        nc.vector.bn_stats(ST[:, b * TPB + u, :], X[:, b * TPB + u, :]).then_inc(stats_done, 1)
                dve.wait_ge(stats_done, TILES)
                ch = Chain(dve, link_sem)
                ch.link(nc.vector.tensor_tensor(A0[:], ST[:, :, 2], ST[:, :, 5], ALU.add))
                ch.link(nc.vector.tensor_tensor(MEAN[:], ST[:, :, 1], ST[:, :, 4], ALU.add))
                ch.link(nc.vector.tensor_tensor(A1[:], ST[:, :, 1], ST[:, :, 4], ALU.subtract))
                ch.link(nc.vector.tensor_scalar(MEAN[:], MEAN[:], 0.5, None, ALU.mult))
                ch.link(nc.vector.tensor_scalar(A0[:], A0[:], 1.0 / D, None, ALU.mult))
                ch.link(nc.vector.tensor_tensor(A1[:], A1[:], A1[:], ALU.mult))
                ch.link(nc.vector.scalar_tensor_tensor(out=VAR[:], in0=A1[:], scalar=0.25, in1=A0[:],
                                                       op0=ALU.mult, op1=ALU.add))
                nc.vector.tensor_scalar(VARE[:], VAR[:], EPS_LN, None, ALU.add).then_inc(var_ready, 1)
                root_vector(dve)

            return MEAN, RSTD, VAR, on_vector, root_scalar

        def experts(k):
            n = f"m{k}_"
            loaded = sem(n + "loaded")
            with ExitStack() as c:
                XN = sb(n + "XN", [P, TILES, D], F32, c)
                SLOT = [sb(f"{n}SLOT{j}", [P, TILES], U32, c) for j in range(2)]
                WT = [sb(f"{n}WT{j}", [P, TILES], F32, c) for j in range(2)]
                EID = sb(n + "EID", [1, SLOT_TILES], I32, c)
                route(k, n, loaded, XN, SLOT, WT, EID)
                run_experts(n, EID)
                combine(n, SLOT, WT)

        def route(k, n, loaded, XN, SLOT, WT, EID):
            with ExitStack() as c:
                MEAN, RSTD, _, ln_vector, ln_scalar = layernorm(n + "ln", c)
                XT = sb(n + "XT", [P, 2, S], F32, c)
                ZERO = sb(n + "ZERO", [P, SLOT_TILES * D // 8], F32, c)
                t8 = lambda s: sb(n + s, [P, TILES, E], F32, c)
                L, L2, Q, ONE1, ONE2, AL, NUM1, NUM2, P1, P2, KEEP, POS = (t8(s) for s in (
                    "L", "L2", "Q", "ONE1", "ONE2", "AL", "NUM1", "NUM2", "P1", "P2", "KEEP", "POS"))
                t1 = lambda s: sb(n + s, [P, TILES], F32, c)
                M1, M2, QM, SUM1, SUM2, SL1, SL2 = (t1(s) for s in ("M1", "M2", "QM", "SUM1", "SUM2", "SL1", "SL2"))
                TOT = sb(n + "TOT", [P, E, TILES], F32, c)
                INCL = sb(n + "INCL", [P, E, TILES], F32, c)
                PADI = sb(n + "PADI", [P, E], I32, c)
                PAD = sb(n + "PAD", [P, E], F32, c)
                END = sb(n + "END", [P, E], F32, c)
                BASE = sb(n + "BASE", [P, E], F32, c)
                CMP = sb(n + "CMP", [1, SLOT_TILES, E], F32, c)
                EF = sb(n + "EF", [1, SLOT_TILES], F32, c)
                TP = [ps(f"{n}TP{h}", [P, S], F32, c) for h in range(2)]
                LG = ps(n + "LG", [P, TILES, E], F32, c)
                RK = ps(n + "RK", [P, 2, TILES, E], F32, c)
                xn_ready, turned, xt_ready, logits_done = (sem(n + s) for s in (
                    "xn_ready", "turned", "xt_ready", "logits_done"))
                num_ready, exp_done, choice_ready, ranks_done, slots_ready = (sem(n + s) for s in (
                    "num_ready", "exp_done", "choice_ready", "ranks_done", "slots_ready"))
                route_link, zero_set, zeroed, scattered = (sem(n + s) for s in (
                    "route_link", "zero_set", "zeroed", "scattered"))
                logits_each = sem(n + "logits_each")
                wide = lambda v: v.unsqueeze(2).broadcast_to([P, TILES, E])
                REV = CT[:, CONST["rev"]].rearrange("p (t e) -> p t e", e=E)

                with nc.Block() as block:
                    @block.sync
                    def _(sp):
                        if k == 0:
                            sp.dma_start(X[:], x_tok).then_inc(loaded, 16)
                            sp.dma_start(CT[:], consts).then_inc(loaded, 16)
                            sp.dma_start(GW[:], gate_w).then_inc(loaded, 16)
                            sp.dma_start(W1[:], w1.rearrange("e p f -> p e f")).then_inc(loaded, 16)
                            sp.dma_start(W3[:], w3.rearrange("e p f -> p e f")).then_inc(loaded, 16)
                            sp.dma_start(W2[:], w2.rearrange("e (c p) d -> p e c d", p=P)).then_inc(loaded, 16)
                            sp.wait_ge(zero_set, 1)
                            rows = XS.rearrange("(g p r) d -> g p (r d)", g=8, p=P)
                            for g in range(8):
                                sp.dma_start(rows[g], ZERO[:]).then_inc(zeroed, 16)
                            sp.dma_start(VEC[:], vecs).then_inc(loaded, 16)
                            sp.wait_ge(loaded, 112)

                    @block.vector
                    def _(dve):
                        if k == 0:
                            nc.vector.memset(ZERO[:], 0.0).then_inc(zero_set, 1)
                            dve.wait_ge(loaded, 112)
                        ln_vector(dve)
                        with dve.Fori(0, B) as b:
                            for u in range(TPB):
                                t = b * TPB + u
                                nc.vector.tensor_scalar(XN[:, t, :], X[:, t, :], MEAN[:, bass.ds(t, 1)],
                                                        RSTD[:, bass.ds(t, 1)], ALU.subtract,
                                                        ALU.mult).then_inc(xn_ready, 1)
                        ch = Chain(dve, route_link)
                        dve.wait_ge(logits_done, 1)
                        ch.link(nc.vector.tensor_copy(L[:], LG[:]))
                        nc.vector.scalar_tensor_tensor(out=AL[:], in0=L[:], scalar=-1.0, in1=L[:], op0=ALU.mult,
                                                       op1=ALU.max)
                        ch.link(nc.vector.tensor_reduce(M1[:], L[:], axis=AX.X, op=ALU.max))

                        def first_of(dst, src, m):
                            ch.link(nc.vector.tensor_tensor(Q[:], src[:], wide(m[:]), ALU.is_equal))
                            ch.link(nc.vector.tensor_tensor(Q[:], Q[:], REV, ALU.mult))
                            ch.link(nc.vector.tensor_reduce(QM[:], Q[:], axis=AX.X, op=ALU.max))
                            ch.link(nc.vector.tensor_tensor(dst[:], Q[:], wide(QM[:]), ALU.is_equal))

                        nc.vector.tensor_tensor(NUM1[:], wide(M1[:]), L[:], ALU.subtract).then_inc(num_ready, 1)
                        first_of(ONE1, L, M1)
                        ch.link(nc.vector.scalar_tensor_tensor(out=L2[:], in0=ONE1[:], scalar=-1e38, in1=L[:],
                                                               op0=ALU.mult, op1=ALU.add))
                        ch.link(nc.vector.tensor_reduce(M2[:], L2[:], axis=AX.X, op=ALU.max))
                        nc.vector.tensor_tensor(NUM2[:], wide(M2[:]), L2[:], ALU.subtract).then_inc(num_ready, 1)
                        first_of(ONE2, L2, M2)
                        ch.link(nc.vector.tensor_tensor(Q[:], ONE1[:], ONE2[:], ALU.add))
                        dve.sem_inc(choice_ready, 1)
                        for j, (m, num, p, s, w) in enumerate(((M1, NUM1, P1, SUM1, WT[0]), (M2, NUM2, P2, SUM2, WT[1]))):
                            ch.link(nc.vector.tensor_tensor(KEEP[:], AL[:], wide(m[:]), ALU.max))
                            ch.link(nc.vector.scalar_tensor_tensor(out=KEEP[:], in0=KEEP[:], scalar=0.02, in1=num[:],
                                                                   op0=ALU.mult, op1=ALU.is_ge))
                            dve.wait_ge(exp_done, j + 1)
                            ch.link(nc.vector.tensor_tensor(KEEP[:], KEEP[:], p[:], ALU.mult))
                            ch.link(nc.vector.tensor_reduce(s[:], KEEP[:], axis=AX.X, op=ALU.add))
                            ch.link(nc.vector.tensor_scalar(s[:], s[:], 2.0, None, ALU.mult))
                            ch.link(nc.vector.reciprocal(w[:], s[:]))
                        dve.wait_ge(ranks_done, 1)
                        ch.link(nc.vector.tensor_copy(TOT[:].rearrange("p e t -> p t e"), RK[:, 1, :, :]))
                        ch.link(nc.vector.tensor_tensor_scan(out=INCL[:].rearrange("p e t -> p (e t)"),
                                                             data0=CT[:, CONST["newexp"]],
                                                             data1=TOT[:].rearrange("p e t -> p (e t)"), initial=0.0,
                                                             op0=ALU.mult, op1=ALU.add))
                        ch.link(nc.vector.tensor_scalar(PADI[:], INCL[:, :, TILES - 1], float(P - 1), None, ALU.add))
                        ch.link(nc.vector.tensor_scalar(PADI[:], PADI[:], -P, None, ALU.bitwise_and))
                        ch.link(nc.vector.tensor_copy(PAD[:], PADI[:]))
                        ch.link(nc.vector.tensor_tensor_scan(out=END[:], data0=CT[:, CONST["ones"]][:, 0:E],
                                                             data1=PAD[:], initial=0.0, op0=ALU.mult, op1=ALU.add))
                        ch.link(nc.vector.tensor_tensor(BASE[:], END[:], PAD[:], ALU.subtract))
                        ch.link(nc.vector.tensor_tensor(INCL[:], INCL[:], TOT[:], ALU.subtract))
                        ch.link(nc.vector.tensor_tensor(INCL[:], INCL[:],
                                                        BASE[:].unsqueeze(2).broadcast_to([P, E, TILES]), ALU.add))
                        ch.link(nc.vector.tensor_tensor(POS[:], INCL[:].rearrange("p e t -> p t e"), RK[:, 0, :, :],
                                                        ALU.add))
                        for one, sl, dst in ((ONE1, SL1, SLOT[0]), (ONE2, SL2, SLOT[1])):
                            ch.link(nc.vector.tensor_tensor(Q[:], one[:], POS[:], ALU.mult))
                            ch.link(nc.vector.tensor_reduce(sl[:], Q[:], axis=AX.X, op=ALU.add))
                            ch.link(nc.vector.tensor_copy(dst[:], sl[:]))
                        dve.sem_inc(slots_ready, 1)
                        ch.link(nc.vector.tensor_tensor(CMP[:],
                                                        END[0:1, :].unsqueeze(1).broadcast_to([1, SLOT_TILES, E]),
                                                        CT[0:1, CONST["tile0"]].unsqueeze(2)
                                                        .broadcast_to([1, SLOT_TILES, E]), ALU.is_le))
                        ch.link(nc.vector.tensor_reduce(EF[:], CMP[:], axis=AX.X, op=ALU.add))
                        ch.link(nc.vector.tensor_scalar(EID[:], EF[:], float(E - 1), None, ALU.min))

                    @block.scalar
                    def _(act):
                        nc.scalar.preload_act_table_set(LN_EXP)
                        ln_scalar(act)
                        with act.Fori(0, B // 2) as i:
                            for h in range(2):
                                act.wait_ge(turned, i * 2 + h + 1)
                                nc.scalar.activation(XT[:, h, :], TP[h][:], ACT.Copy).then_inc(xt_ready, 1)
                        for j, (num, p) in enumerate(((NUM1, P1), (NUM2, P2))):
                            act.wait_ge(num_ready, j + 1)
                            nc.scalar.activation(p[:], num[:], ACT.Exp, scale=-1.0).then_inc(exp_done, 1)

                    @block.tensor
                    def _(pe):
                        if k == 0:
                            pe.wait_ge(loaded, 112)
                        for i in range(B // 2):
                            for h in range(2):
                                b = i * 2 + h
                                pe.wait_ge(xn_ready, b * TPB + TPB)
                                for u in range(TPB):
                                    last = nc.tensor.transpose(TP[h][:, u * P:(u + 1) * P], XN[:, b * TPB + u, :],
                                                               IDENT)
                                last.then_inc(turned, 1)
                                pe.wait_ge(xt_ready, b + 1)
                                for u in range(TPB):
                                    last = nc.tensor.matmul(LG[:, b * TPB + u, :], XT[:, h, u * P:(u + 1) * P], GW[:],
                                                            start=True, stop=True)
                                last.then_inc(logits_each, 1)
                        pe.wait_ge(logits_each, B)
                        pe.sem_inc(logits_done, 1)
                        pe.wait_ge(choice_ready, 1)
                        q = Q[:].rearrange("p t e -> p (t e)")
                        nc.tensor.matmul(RK[:, 0, :, :].rearrange("p t e -> p (t e)"), BEFORE, q, start=True, stop=True)
                        nc.tensor.matmul(RK[:, 1, :, :].rearrange("p t e -> p (t e)"), ONES, q, start=True,
                                         stop=True).then_inc(ranks_done, 1)

                    @block.gpsimd
                    def _(pool):
                        if k == 0:
                            pool.wait_ge(zeroed, 128)
                        pool.wait_ge(slots_ready, 1)
                        for t in range(TILES):
                            for j in range(2):
                                nc.gpsimd.indirect_dma_start(
                                    XS, bass.IndirectOffsetOnAxis(ap=SLOT[j][:, t:t + 1], axis=0), XN[:, t, :],
                                    None).then_inc(scattered, 16)
                        pool.wait_ge(scattered, 16 * 2 * TILES)

        def run_experts(n, EID):
            IN, OUT = 4, 4
            with ExitStack() as c:
                XB = sb(n + "XB", [P, IN, D], F32, c)
                XT = sb(n + "XTs", [P, 2, P], F32, c)
                G = sb(n + "G", [P, 2, FF], F32, c)
                H = sb(n + "H", [P, 2, FF], F32, c)
                HT = sb(n + "HT", [P, 2, FF], F32, c)
                Y = sb(n + "Y", [P, OUT, D], F32, c)
                gp = [ps(f"{n}gp{h}", [P, FF], F32, c) for h in range(2)]
                up = [ps(f"{n}up{h}", [P, FF], F32, c) for h in range(2)]
                hp = [ps(f"{n}hp{h}", [P, FF], F32, c) for h in range(2)]
                xp = ps(n + "xp", [P, FF], F32, c)
                yp = ps(n + "yp", [P, FF], F32, c)
                rows_in = [sem(f"{n}rows_in{u}") for u in range(IN)]
                rows_out = [sem(f"{n}rows_out{u}") for u in range(OUT)]
                x_turned, xt_ready, g_done, silu_done, u_done, h_ready = (sem(n + s) for s in (
                    "x_turned", "xt_ready2", "g_done", "silu_done", "u_done", "h_ready"))
                h_turned, ht_ready, y_done, y_ready = (sem(n + s) for s in ("h_turned", "ht_ready", "y_done", "y_ready"))
                xs_t = XS.rearrange("(i p) d -> p i d", p=P)
                ys_t = YS.rearrange("(i p) d -> p i d", p=P)
                STEPS = SLOT_TILES // 4

                def wait(eng, s, v, known):
                    if not isinstance(known, int) or known > 0:
                        eng.wait_ge(s, v)

                def loop(eng, step):
                    for u in range(4):
                        step(u, u, u, False)
                    with eng.Fori(1, STEPS - 1) as it:
                        for u in range(4):
                            step(it * 4 + u, u, None, False)
                    for u in range(4):
                        step((STEPS - 1) * 4 + u, u, None, u == 3)

                with nc.Block() as block:
                    @block.sync
                    def _(sp):
                        for u in range(IN):
                            sp.dma_start(XB[:, u, :], xs_t[:, u, :]).then_inc(rows_in[u], 16)

                        def step(i, u, more):
                            if more:
                                sp.wait_ge(x_turned, i + 1)
                                sp.dma_start(XB[:, u, :], xs_t[:, i + IN, :]).then_inc(rows_in[u], 16)
                            sp.wait_ge(y_ready, i + 1)
                            sp.dma_start(ys_t[:, i, :], Y[:, u, :]).then_inc(rows_out[u], 16)

                        with sp.Fori(0, STEPS - 1) as it:
                            for u in range(4):
                                step(it * 4 + u, u, True)
                        for u in range(4):
                            step((STEPS - 1) * 4 + u, u, False)
                        for u in range(OUT):
                            sp.wait_ge(rows_out[u], 16 * STEPS)

                    @block.vector
                    def _(dve):
                        def turn_x(i, u, first):
                            dve.wait_ge(x_turned, i + 1)
                            if first is None or first >= 2:
                                dve.wait_ge(u_done, i - 1)
                            nc.vector.tensor_copy(XT[:, u % 2, :], xp[:, 0:P]).then_inc(xt_ready, 1)

                        turn_x(0, 0, 0)

                        def step(i, u, first, last):
                            if not last:
                                turn_x(i + 1, u + 1, None if first is None else first + 1)
                            dve.wait_ge(silu_done, i + 1)
                            dve.wait_ge(u_done, i + 1)
                            if first is None or first >= 2:
                                dve.wait_ge(h_turned, i - 1)
                            nc.vector.tensor_tensor(H[:, u % 2, :], up[u % 2][:], G[:, u % 2, :],
                                                    ALU.mult).then_inc(h_ready, 1)

                        loop(dve, step)

                    @block.scalar
                    def _(act):
                        nc.scalar.preload_act_table(ACT.Silu)

                        def down(i, u, first):
                            h = u % 2
                            act.wait_ge(h_turned, i + 1)
                            if first is None or first >= 2:
                                act.wait_ge(y_done, i - 1)
                            nc.scalar.activation(HT[:, h, :], hp[h][:], ACT.Copy).then_inc(ht_ready, 1)
                            act.wait_ge(y_done, i + 1)
                            if first is None:
                                act.wait_ge(rows_out[u % 4], (i // 4) * 16 if isinstance(i, int) else (i - u) * 4)
                            nc.scalar.activation(Y[:, u % 4, :], yp[:, 0:D], ACT.Copy).then_inc(y_ready, 1)

                        def step(i, u, first, last):
                            act.wait_ge(g_done, i + 1)
                            if first is None or first >= 2:
                                act.wait_ge(h_ready, i - 1)
                            nc.scalar.activation(G[:, u % 2, :], gp[u % 2][:], ACT.Silu).then_inc(silu_done, 1)
                            if first is None:
                                down_prev(i, u)
                            elif first > 0:
                                down(i - 1, u - 1, first - 1)

                        def down_prev(i, u):
                            j = i - 1
                            v = (u - 1) % 4
                            act.wait_ge(h_turned, j + 1)
                            act.wait_ge(y_done, j - 1)
                            nc.scalar.activation(HT[:, v % 2, :], hp[v % 2][:], ACT.Copy).then_inc(ht_ready, 1)
                            act.wait_ge(y_done, j + 1)
                            base = i - u
                            rounds = base if u > 0 else base - 4
                            if isinstance(rounds, int):
                                if rounds > 0:
                                    act.wait_ge(rows_out[v], rounds * 4)
                            else:
                                act.wait_ge(rows_out[v], rounds * 4) if u > 0 else act.wait_ge(rows_out[v], base * 4 - 16)
                            nc.scalar.activation(Y[:, v, :], yp[:, 0:D], ACT.Copy).then_inc(y_ready, 1)

                        loop(act, step)
                        i = SLOT_TILES
                        down_prev(i, 0)

                    @block.tensor
                    def _(pe):
                        def turn_x(i, u, first):
                            pe.wait_ge(rows_in[u % 4], 16 * (i // 4 + 1) if isinstance(i, int) else (i - u) * 4 + 16)
                            if first is None or first >= 1:
                                pe.wait_ge(xt_ready, i)
                            nc.tensor.transpose(xp[:, 0:P], XB[:, u % 4, :], IDENT).then_inc(x_turned, 1)

                        def turn_next(i, u, first):
                            v = (u + 1) % 4
                            if isinstance(i, int):
                                pe.wait_ge(rows_in[v], 16 * ((i + 1) // 4 + 1))
                            else:
                                pe.wait_ge(rows_in[v], (i - u) * 4 + (16 if u < 3 else 32))
                            pe.wait_ge(xt_ready, i + 1)
                            nc.tensor.transpose(xp[:, 0:P], XB[:, v, :], IDENT).then_inc(x_turned, 1)

                        def turn_h(j, h, first):
                            pe.wait_ge(h_ready, j + 1)
                            if first is None or first >= 2:
                                pe.wait_ge(ht_ready, j - 1)
                            for f in range(FC):
                                last = nc.tensor.transpose(hp[h][:, f * P:(f + 1) * P], H[:, h, f * P:(f + 1) * P],
                                                           IDENT)
                            last.then_inc(h_turned, 1)

                        def down(j, h, first):
                            e = pe.value_load(EID[0:1, bass.ds(j, 1)], min_val=0, max_val=E - 1)
                            pe.wait_ge(ht_ready, j + 1)
                            if first is None or first >= 1:
                                pe.wait_ge(y_ready, j)
                            for f in range(FC):
                                last = nc.tensor.matmul(yp[:, 0:D], HT[:, h, f * P:(f + 1) * P],
                                                        W2[:, bass.ds(e, 1), f, :], start=(f == 0), stop=(f == FC - 1))
                            last.then_inc(y_done, 1)

                        turn_x(0, 0, 0)

                        def step(i, u, first, last):
                            h = u % 2
                            prev = None if first is None else first - 1
                            e = pe.value_load(EID[0:1, bass.ds(i, 1)], min_val=0, max_val=E - 1)
                            pe.wait_ge(xt_ready, i + 1)
                            if first is None or first >= 2:
                                pe.wait_ge(silu_done, i - 1)
                            nc.tensor.matmul(gp[h][:], XT[:, h, :], W1[:, bass.ds(e, 1), :], start=True,
                                             stop=True).then_inc(g_done, 1)
                            if first is None or first >= 1:
                                turn_h(i - 1, 1 - h, prev)
                            if first is None or first >= 2:
                                pe.wait_ge(h_ready, i - 1)
                            nc.tensor.matmul(up[h][:], XT[:, h, :], W3[:, bass.ds(e, 1), :], start=True,
                                             stop=True).then_inc(u_done, 1)
                            if not last:
                                turn_next(i, u, first)
                            if first is None or first >= 1:
                                down(i - 1, 1 - h, prev)

                        loop(pe, step)
                        turn_h(SLOT_TILES - 1, 1, None)
                        down(SLOT_TILES - 1, 1, None)

        def combine(n, SLOT, WT):
            BUF = 8
            with ExitStack() as c:
                GB = sb(n + "GB", [P, BUF, D], F32, c)
                ACC = sb(n + "ACC", [P, BUF // 2, D], F32, c)
                fetched = [sem(f"{n}fetched{u}") for u in range(BUF)]
                half_sum, added = sem(n + "half_sum"), sem(n + "added")
                with nc.Block() as block:
                    @block.gpsimd
                    def _(pool):
                        for t in range(TILES):
                            for j in range(2):
                                i = 2 * t + j
                                if i >= BUF:
                                    (pool.wait_ge(half_sum, t - BUF // 2 + 1) if j == 0 else
                                     pool.wait_ge(added, t - BUF // 2 + 1))
                                nc.gpsimd.indirect_dma_start(
                                    GB[:, i % BUF, :], None, YS,
                                    bass.IndirectOffsetOnAxis(ap=SLOT[j][:, t:t + 1], axis=0)).then_inc(
                                        fetched[i % BUF], 16)

                    @block.vector
                    def _(dve):
                        with dve.Fori(0, TILES // 4) as r:
                            for u in range(4):
                                t = r * 4 + u
                                dve.wait_ge(fetched[2 * u], r * 16 + 16)
                                nc.vector.scalar_tensor_tensor(
                                    out=ACC[:, u, :], in0=GB[:, 2 * u, :], scalar=WT[0][:, bass.ds(t, 1)],
                                    in1=X[:, t, :], op0=ALU.mult, op1=ALU.add).then_inc(half_sum, 1)
                                dve.wait_ge(fetched[2 * u + 1], r * 16 + 16)
                                dve.wait_ge(half_sum, t + 1)
                                nc.vector.scalar_tensor_tensor(
                                    out=X[:, t, :], in0=GB[:, 2 * u + 1, :], scalar=WT[1][:, bass.ds(t, 1)],
                                    in1=ACC[:, u, :], op0=ALU.mult, op1=ALU.add).then_inc(added, 1)
                        dve.wait_ge(added, TILES)

        def scan_layer():
            n = "s_"
            with ExitStack() as c:
                MEAN, RSTD, VAR, ln_vector, ln_scalar = layernorm(n + "ln", c)
                tile = lambda name, shape: sb(n + name, shape, F32, c)
                MS, RMS, R2, R1P, MR = (tile(s, [P, TILES]) for s in ("MS", "RMS", "R2", "R1P", "MR"))
                ms_ready, rms_vector, rms_scalar = rsqrt(n + "rms", MS[:], RMS[:], c)
                CONVD, INP = tile("CONVD", [P, KC, P]), tile("INP", [P, 4, P])
                MIX, OUTP = tile("MIX", [P, P]), tile("OUTP", [P, P])
                XN = tile("XN", [P, 2, TPB, D])
                CV = tile("CV", [P, 2, KC - 1 + S])
                XC = tile("XC", [P, 2, S])
                wide = lambda name: tile(name, [P, S])
                SC, EDT, EDT1, LDT, DT, GATE, ROT1, ROT2, ROT, VIN, LD, LS, E1, E2, TV, CS, CK, FIN, FG = (
                    wide(s) for s in ("SC", "EDT", "EDT1", "LDT", "DT", "GATE", "ROT1", "ROT2",
                                      "ROT", "VIN", "LD", "LS", "E1", "E2", "TV", "CS", "CK", "FIN", "FG"))
                small = lambda name: tile(name, [P, CHUNKS])
                BOUT, LAST, CD, NCD, EN, EP, FIRST, SEED, SUM, CARRY = (small(s) for s in (
                    "BOUT", "LAST", "CD", "NCD", "EN", "EP", "FIRST", "SEED", "SUM", "CARRY"))
                tp, cv, pdt, pv, pvs, pg, mp, op = (ps(n + s, [P, S], F32, c) for s in (
                    "tp", "cv", "pdt", "pv", "pvs", "pg", "mp", "op"))
                (weights_in, pads_set, scalars_ready, xn_ready, turned, scaled, clipped, conv_done, conv_sig,
                 xc_ready, proj_done, x_plus, dt_exp, dt_low, dt_ln, dt_ready, gate_ready,
                 turned_v, vin_ready, ls_ready, e_ready, cs_ready, small_ready, small_exp, fin_ready, mixed, fg_ready,
                 projected, x_done, chain_b, chain_p, chain_0) = (sem(n + s) for s in (
                    "weights_in", "pads_set", "scalars_ready", "xn_ready", "turned", "scaled", "clipped", "conv_done",
                    "conv_sig", "xc_ready", "proj_done", "x_plus", "dt_exp", "dt_low", "dt_ln", "dt_ready", "gate_ready", "turned_v", "vin_ready", "ls_ready", "e_ready", "cs_ready", "small_ready",
                    "small_exp", "fin_ready", "mixed", "fg_ready", "projected", "x_done", "chain_b",
                    "chain_p", "chain_0"))
                by_chunk = lambda v: v.rearrange("p (c n) -> p c n", n=CHUNK)
                spread = lambda v: v.unsqueeze(2).broadcast_to([P, CHUNKS, CHUNK])
                NEWCHUNK = CT[:, CONST["newchunk"]]

                with nc.Block() as block:
                    @block.sync
                    def _(sp):
                        sp.dma_start(CONVD[:], conv_diag).then_inc(weights_in, 16)
                        sp.dma_start(INP[:], in_proj).then_inc(weights_in, 16)
                        sp.dma_start(MIX[:], head_mix).then_inc(weights_in, 16)
                        sp.dma_start(OUTP[:], out_proj).then_inc(weights_in, 16)
                        sp.wait_ge(weights_in, 64)

                    @block.vector
                    def _(dve):
                        nc.vector.memset(CV[:, :, 0:KC - 1], 0.0).then_inc(pads_set, 1)
                        nc.vector.memset(CARRY[:, 0:1], 0.0).then_inc(pads_set, 1)
                        ln_vector(dve)
                        ch = Chain(dve, chain_0)
                        ch.link(nc.vector.tensor_tensor(R1P[:], RSTD[:], RSTD[:], ALU.mult))
                        ch.link(nc.vector.tensor_tensor(MS[:], VAR[:], R1P[:], ALU.mult))
                        nc.vector.tensor_scalar(MS[:], MS[:], EPS_RMS, None, ALU.add).then_inc(ms_ready, 1)
                        ch.link(nc.vector.tensor_scalar(R1P[:], RSTD[:], 1.0, None, ALU.add))
                        ch.link(nc.vector.scalar_tensor_tensor(out=MR[:], in0=MEAN[:], scalar=-1.0, in1=RSTD[:],
                                                               op0=ALU.mult, op1=ALU.mult))
                        rms_vector(dve)
                        ch.link(nc.vector.tensor_tensor(R2[:], RSTD[:], RMS[:], ALU.mult))
                        dve.sem_inc(scalars_ready, 1)

                        NB = 13

                        def body(b, h, a):
                            ah = 1 - h
                            if a is not None:
                                some_wait(dve, turned, a - 1)
                                for u in range(TPB):
                                    t = a * TPB + u
                                    nc.vector.tensor_scalar(XN[:, ah, u, :], X[:, bass.ds(t, 1), :],
                                                            MEAN[:, bass.ds(t, 1)], R2[:, bass.ds(t, 1)],
                                                            ALU.subtract, ALU.mult).then_inc(xn_ready, 1)
                            if b is not None:
                                cb = Chain(dve, chain_b, b * NB)
                                dve.wait_ge(dt_exp, b + 1)
                                nc.vector.tensor_scalar(EDT1[:], EDT[:], 1e4, 1.0, ALU.min, ALU.add).then_inc(dt_low, 1)
                                some_wait(dve, vin_ready, b)
                                nc.vector.tensor_tensor(ROT1[:], pv[:], CT[:, CONST["cos"]],
                                                        ALU.mult).then_inc(turned_v, 1)
                                nc.vector.tensor_tensor(ROT2[:], pvs[:], CT[:, CONST["sin"]],
                                                        ALU.mult).then_inc(turned_v, 1)
                            if a is not None:
                                dve.wait_ge(scaled, a + 1)
                                nc.vector.tensor_scalar(CV[:, ah, KC - 1:], CV[:, ah, KC - 1:], 60000.0, -60000.0,
                                                        ALU.min, ALU.max).then_inc(clipped, 1)
                            if b is not None:
                                dve.wait_ge(dt_ln, b + 1)
                                nc.vector.tensor_scalar(DT[:], LDT[:], 0.001, 2.0, ALU.max, ALU.min).then_inc(dt_ready, 1)
                                dve.wait_ge(dt_ready, b + 1)
                                cb.link(nc.vector.tensor_tensor_scan(out=LD[:], data0=NEWCHUNK, data1=DT[:],
                                                                     initial=0.0, op0=ALU.mult, op1=ALU.add))
                                cb.link(nc.vector.tensor_scalar(LD[:], LD[:], 20.0, None, ALU.min))
                                nc.vector.tensor_tensor(by_chunk(LS[:]), by_chunk(LD[:]),
                                                        by_chunk(LD[:])[:, :, 0:1].broadcast_to([P, CHUNKS, CHUNK]),
                                                        ALU.subtract).then_inc(ls_ready, 1)
                                cb.link(nc.vector.tensor_copy(LAST[:], by_chunk(LD[:])[:, :, CHUNK - 1]))
                                cb.link(nc.vector.tensor_tensor_scan(
                                    out=CD[:], data0=CT[:, CONST["ones"]][:, 0:CHUNKS], data1=LAST[:], initial=0.0,
                                    op0=ALU.mult, op1=ALU.add))
                                cb.link(nc.vector.tensor_scalar(CD[:], CD[:], 80.0, None, ALU.min))
                                nc.vector.tensor_scalar(NCD[:], CD[:], CD[:, 0:1], 20.0, ALU.subtract,
                                                        ALU.min).then_inc(small_ready, 1)
                            if b is not None:
                                dve.wait_ge(e_ready, b + 1)
                                dve.wait_ge(vin_ready, b + 1)
                                cb.link(nc.vector.tensor_tensor(TV[:], E1[:], VIN[:], ALU.mult))
                                cb.link(nc.vector.tensor_tensor_scan(out=CS[:], data0=NEWCHUNK, data1=TV[:],
                                                                     initial=0.0, op0=ALU.mult, op1=ALU.add))
                                cb.link(nc.vector.tensor_tensor(BOUT[:], by_chunk(CS[:])[:, :, CHUNK - 1],
                                                                by_chunk(E2[:])[:, :, CHUNK - 1], ALU.mult))
                                dve.wait_ge(small_exp, b + 1)
                                cb.link(nc.vector.tensor_tensor(SEED[:], BOUT[:], EN[:], ALU.mult))
                                cb.link(nc.vector.tensor_tensor_scan(
                                    out=SUM[:], data0=CT[:, CONST["ones"]][:, 0:CHUNKS], data1=SEED[:], initial=0.0,
                                    op0=ALU.mult, op1=ALU.add))
                                cb.link(nc.vector.tensor_tensor(CARRY[:, 1:], SUM[:, 0:CHUNKS - 1], EP[:, 1:], ALU.mult))
                                cb.link(nc.vector.tensor_tensor(CARRY[:, 1:], CARRY[:, 1:], FIRST[:, 1:], ALU.mult))
                                cb.link(nc.vector.tensor_tensor(by_chunk(CK[:]), by_chunk(CS[:]), spread(CARRY[:]),
                                                                ALU.add))
                                nc.vector.tensor_tensor(FIN[:], E2[:], CK[:], ALU.mult).then_inc(fin_ready, 1)
                            if a is not None:
                                dve.wait_ge(conv_sig, a + 1)
                                some_wait(dve, proj_done, a - 1)
                                nc.vector.scalar_tensor_tensor(out=XC[:, ah, :], in0=cv[:], scalar=CONV_B, in1=SC[:],
                                                               op0=ALU.add, op1=ALU.mult).then_inc(xc_ready, 1)
                            if b is not None:
                                dve.wait_ge(mixed, b + 1)
                                dve.wait_ge(gate_ready, b + 1)
                                some_wait(dve, projected, b)
                                nc.vector.tensor_tensor(FG[:], mp[:], GATE[:], ALU.mult).then_inc(fg_ready, 1)
                                dve.wait_ge(projected, b + 1)
                                dve.wait_ge(x_plus, b * TPB + TPB)
                                xb = X[:, bass.ds(b * TPB, TPB), :].rearrange("p t d -> p (t d)")
                                nc.vector.tensor_tensor(xb, op[:], xb, ALU.add).then_inc(x_done, 1)
                                assert cb.n == NB, cb.n

                        over_batches(dve, body)
                        dve.wait_ge(x_done, B)

                    @block.scalar
                    def _(act):
                        nc.scalar.preload_act_table_set(LN_EXP)
                        ln_scalar(act)
                        rms_scalar(act)
                        act.wait_ge(scalars_ready, 1)
                        act.wait_ge(pads_set, 2)

                        def body(b, h, a):
                            ah = 1 - h
                            if b is not None:
                                act.wait_ge(proj_done, b + 1)
                                some_wait(act, dt_low, b)
                                nc.scalar.activation(EDT[:], pdt[:], ACT.Exp, bias=DT_BIAS).then_inc(dt_exp, 1)
                            if a is not None:
                                act.wait_ge(xn_ready, a * TPB + TPB)
                                for u in range(TPB):
                                    t = a * TPB + u
                                    nc.scalar.activation(X[:, bass.ds(t, 1), :], X[:, bass.ds(t, 1), :], ACT.Identity,
                                                         scale=R1P[:, bass.ds(t, 1)],
                                                         bias=MR[:, bass.ds(t, 1)]).then_inc(x_plus, 1)
                                act.wait_ge(turned, a + 1)
                                some_wait(act, conv_done, a - 1)
                                nc.scalar.activation(CV[:, ah, KC - 1:], tp[:], ACT.Identity,
                                                     scale=NORM_SCALE).then_inc(scaled, 1)
                            if b is not None:
                                act.wait_ge(dt_low, b + 1)
                                some_wait(act, dt_ready, b)
                                nc.scalar.activation(LDT[:], EDT1[:], ACT.Ln).then_inc(dt_ln, 1)
                            if b is not None:
                                act.wait_ge(ls_ready, b + 1)
                                some_wait(act, fin_ready, b)
                                nc.scalar.activation(E1[:], LS[:], ACT.Exp)
                                nc.scalar.activation(E2[:], LS[:], ACT.Exp, scale=-1.0).then_inc(e_ready, 1)
                                act.wait_ge(small_ready, b + 1)
                                nc.scalar.activation(FIRST[:], by_chunk(LD[:])[:, :, 0], ACT.Exp, scale=-1.0)
                                nc.scalar.activation(EN[:], NCD[:], ACT.Exp)
                                nc.scalar.activation(EP[:], NCD[:], ACT.Exp, scale=-1.0).then_inc(small_exp, 1)
                                some_wait(act, fg_ready, b)
                                nc.scalar.activation(GATE[:], pg[:], ACT.Sigmoid).then_inc(gate_ready, 1)
                            if a is not None:
                                act.wait_ge(conv_done, a + 1)
                                some_wait(act, xc_ready, a)
                                nc.scalar.activation(SC[:], cv[:], ACT.Sigmoid, bias=CONV_B).then_inc(conv_sig, 1)
                            nc.scalar.preload_act_table_set(LN_EXP)

                        over_batches(act, body)

                    @block.gpsimd
                    def _(pool):
                        def body(b, h, a):
                            if b is not None:
                                pool.wait_ge(turned_v, 2 * b + 2)
                                nc.gpsimd.tensor_tensor(ROT[:], ROT1[:], ROT2[:], ALU.add).then_inc(chain_p, 1)
                                pool.wait_ge(chain_p, b + 1)
                                pool.wait_ge(dt_ready, b + 1)
                                nc.gpsimd.tensor_tensor(VIN[:], ROT[:], DT[:], ALU.mult).then_inc(vin_ready, 1)

                        over_batches(pool, body)

                    @block.tensor
                    def _(pe):
                        pe.wait_ge(weights_in, 64)

                        def body(b, h, a):
                            ah = 1 - h
                            if a is not None:
                                pe.wait_ge(xn_ready, a * TPB + TPB)
                                some_wait(pe, scaled, a)
                                for u in range(TPB):
                                    last = nc.tensor.transpose(tp[:, u * P:(u + 1) * P], XN[:, ah, u, :], IDENT)
                                last.then_inc(turned, 1)
                                pe.wait_ge(clipped, a + 1)
                                some_wait(pe, xc_ready, a)
                                for w in range(KC):
                                    last = nc.tensor.matmul(cv[:], CONVD[:, w, :], CV[:, ah, w:w + S], start=(w == 0),
                                                            stop=(w == KC - 1))
                                last.then_inc(conv_done, 1)
                                pe.wait_ge(xc_ready, a + 1)
                                some_wait(pe, dt_exp, a)
                                some_wait(pe, gate_ready, a)
                                some_wait(pe, turned_v, 2 * a)
                                for w, bank in enumerate((pdt, pg, pv, pvs)):
                                    last = nc.tensor.matmul(bank[:], INP[:, w, :], XC[:, ah, :], start=True, stop=True)
                                last.then_inc(proj_done, 1)
                            if b is not None:
                                pe.wait_ge(fin_ready, b + 1)
                                some_wait(pe, fg_ready, b)
                                nc.tensor.matmul(mp[:], MIX[:], FIN[:], start=True, stop=True).then_inc(mixed, 1)
                                pe.wait_ge(fg_ready, b + 1)
                                some_wait(pe, x_done, b)
                                for u in range(TPB):
                                    last = nc.tensor.matmul(op[:, u * P:(u + 1) * P], FG[:, u * P:(u + 1) * P],
                                                            OUTP[:], start=True, stop=True)
                                last.then_inc(projected, 1)

                        over_batches(pe, body)

        def shifted_ffn(k):
            n = f"f{k}_"
            with ExitStack() as c:
                MEAN, RSTD, _, ln_vector, ln_scalar = layernorm(n + "ln", c)
                tile = lambda name, shape: sb(n + name, shape, F32, c)
                FW = tile("FW", [P, 3, P])
                WR, WK = tile("WR", [P, 2, P]), tile("WK", [P, 2, P])
                XN = tile("XN", [P, 2, TPB, D])
                Z = tile("Z", [P, 2, 1 + S])
                KR, KA, TMP = (tile(s, [P, S]) for s in ("KR", "KA", "TMP"))
                R = tile("R", [P, 2, S])
                tp, kp, rp, vp = (ps(n + s, [P, S], F32, c) for s in ("tp", "kp", "rp", "vp"))
                (weights_in, w_ready, pads_set, xn_ready, turned, z_ready, kr_done, k_relu, ka_ready, r_ready,
                 v_done, x_done, chain_b, chain_0) = (sem(n + s) for s in (
                    "weights_in", "w_ready", "pads_set", "xn_ready", "turned", "z_ready", "kr_done", "k_relu",
                    "ka_ready", "r_ready", "v_done", "x_done", "chain_b", "chain_0"))

                with nc.Block() as block:
                    @block.sync
                    def _(sp):
                        sp.dma_start(FW[:], ffn_w).then_inc(weights_in, 16)
                        sp.wait_ge(weights_in, 16)

                    @block.vector
                    def _(dve):
                        nc.vector.memset(Z[:, :, 0:1], 0.0).then_inc(pads_set, 1)
                        dve.wait_ge(weights_in, 16)
                        ch = Chain(dve, chain_0)
                        ch.link(nc.vector.tensor_scalar(VEC[:, 5:7], VEC[:, 3:5], -1.0, 1.0, ALU.mult, ALU.add))
                        for w, (dst, mu) in enumerate(((WR, MU_R), (WK, MU_K))):
                            nc.vector.tensor_scalar(dst[:, 0, :], FW[:, w, :], mu, None, ALU.mult).then_inc(w_ready, 1)
                            nc.vector.tensor_scalar(dst[:, 1, :], FW[:, w, :], VEC[:, 5 + w:6 + w], None,
                                                    ALU.mult).then_inc(w_ready, 1)
                        ln_vector(dve)

                        def body(b, h, a):
                            ah = 1 - h
                            if a is not None:
                                some_wait(dve, turned, a - 1)
                                for u in range(TPB):
                                    t = a * TPB + u
                                    nc.vector.tensor_scalar(XN[:, ah, u, :], X[:, bass.ds(t, 1), :],
                                                            MEAN[:, bass.ds(t, 1)], RSTD[:, bass.ds(t, 1)],
                                                            ALU.subtract, ALU.mult).then_inc(xn_ready, 1)
                            if b is not None:
                                cb = Chain(dve, chain_b, b * 1)
                                dve.wait_ge(k_relu, b + 1)
                                some_wait(dve, v_done, b)
                                nc.vector.tensor_tensor(KA[:], kp[:], KR[:], ALU.mult).then_inc(ka_ready, 1)
                                dve.wait_ge(r_ready, b + 1)
                                dve.wait_ge(v_done, b + 1)
                                cb.link(nc.vector.scalar_tensor_tensor(out=TMP[:], in0=vp[:], scalar=0.5, in1=R[:, h, :],
                                                                       op0=ALU.mult, op1=ALU.mult))
                                xb = X[:, bass.ds(b * TPB, TPB), :].rearrange("p t d -> p (t d)")
                                nc.vector.tensor_tensor(xb, xb, TMP[:], ALU.add).then_inc(x_done, 1)

                        over_batches(dve, body)
                        dve.wait_ge(x_done, B)

                    @block.scalar
                    def _(act):
                        nc.scalar.preload_act_table_set(LN_EXP)
                        ln_scalar(act)
                        nc.scalar.preload_act_table(ACT.Sigmoid)
                        act.wait_ge(pads_set, 1)

                        def body(b, h, a):
                            ah = 1 - h
                            if a is not None:
                                act.wait_ge(turned, a + 1)
                                some_wait(act, kr_done, a - 1)
                                nc.scalar.activation(Z[:, ah, 1:], tp[:], ACT.Copy).then_inc(z_ready, 1)
                            if b is not None:
                                act.wait_ge(kr_done, b + 1)
                                some_wait(act, ka_ready, b)
                                nc.scalar.activation(KR[:], kp[:], ACT.Relu).then_inc(k_relu, 1)
                                some_wait(act, x_done, b - 1)
                                nc.scalar.activation(R[:, h, :], rp[:], ACT.Sigmoid).then_inc(r_ready, 1)

                        over_batches(act, body)

                    @block.tensor
                    def _(pe):
                        pe.wait_ge(w_ready, 4)

                        def body(b, h, a):
                            ah = 1 - h
                            if a is not None:
                                pe.wait_ge(xn_ready, a * TPB + TPB)
                                some_wait(pe, z_ready, a)
                                for u in range(TPB):
                                    last = nc.tensor.transpose(tp[:, u * P:(u + 1) * P], XN[:, ah, u, :], IDENT)
                                last.then_inc(turned, 1)
                            if b is not None:
                                pe.wait_ge(z_ready, b + 1)
                                some_wait(pe, ka_ready, b)
                                some_wait(pe, r_ready, b)
                                nc.tensor.matmul(kp[:], WK[:, 0, :], Z[:, h, 1:], start=True, stop=False)
                                nc.tensor.matmul(kp[:], WK[:, 1, :], Z[:, h, 0:S], start=False, stop=True)
                                for u in range(TPB):
                                    nc.tensor.matmul(rp[:, u * P:(u + 1) * P], Z[:, h, 1 + u * P:1 + (u + 1) * P],
                                                     WR[:, 0, :], start=True, stop=False)
                                    last = nc.tensor.matmul(rp[:, u * P:(u + 1) * P], Z[:, h, u * P:(u + 1) * P],
                                                            WR[:, 1, :], start=False, stop=True)
                                last.then_inc(kr_done, 1)
                                pe.wait_ge(ka_ready, b + 1)
                                some_wait(pe, x_done, b)
                                for u in range(TPB):
                                    last = nc.tensor.matmul(vp[:, u * P:(u + 1) * P], KA[:, u * P:(u + 1) * P],
                                                            FW[:, 2, :], start=True, stop=True)
                                last.then_inc(v_done, 1)

                        over_batches(pe, body)

        def attention():
            n = "a_"
            STEPS = B * GROUPS
            QUNITS = [(3, j, 1, 4 * P) for j in range(4)] + [(2, j, 1, 3 * P) for j in range(4)] + \
                     [(1, 0, 2, 2 * P), (1, 2, 2, 2 * P), (0, 0, 4, P)]
            KUNITS = [(TPB - 1 - qt, j, m, w) for qt, j, m, w in QUNITS]
            KOFF = [0, 4 * P, 7 * P, 9 * P]
            SCALE = 1.0 / math.sqrt(DK)
            NU = len(QUNITS)
            SR, TR = 3, 2
            with ExitStack() as c:
                MEAN, RSTD, _, ln_vector, ln_scalar = layernorm(n + "ln", c)
                tile = lambda name, shape, dt=F32: sb(n + name, shape, dt, c)
                WQ, WK = tile("WQ", [P, GROUPS, P]), tile("WK", [P, GROUPS, P])
                WV, WO = tile("WV", [P, P]), tile("WO", [P, P])
                MASKF, MASK = tile("MASKF", [P, 3, P]), tile("MASK", [P, 3, P], BF16)
                XN, Z = tile("XN", [P, TPB, D]), tile("Z", [P, S])
                PART = tile("PART", [P, S], F32R)
                Q = tile("Q", [P, 2, GROUPS, S], F32R)
                K = tile("K", [P, GROUPS, S], F32R)
                KPAD = tile("KPAD", [P, 2, HA, S], F32R)
                V = tile("V", [P, 2, TPB, HA, QR])
                QM = tile("QM", [P, 2, S], F32R)
                NMAX = tile("NMAX", [P, 2, TPB, GH])
                NHIGH = tile("NHIGH", [P, TPB, GH], F32R)
                SPREAD = tile("SPREAD", [P, TPB, P])
                PT = tile("PT", [P, 2, GH, 10 * P])
                CTX = tile("CTX", [P, S])
                RSUM = tile("RSUM", [P, TPB, GH])
                CN = tile("CN", [P, TPB, P])
                CNT = tile("CNT", [P, S])
                score = [ps(f"{n}score{i}", [P, S], F32, c) for i in range(SR)]
                scoret = [ps(f"{n}scoret{i}", [P, S], F32, c) for i in range(TR)]
                ctxp, mixp, turnp = (ps(n + s, [P, S], F32, c) for s in ("ctxp", "mixp", "turnp"))
                names = ("weights_in", "zeros_set", "mask_ready", "xn_ready", "turned", "z_ready", "v_done", "v_ready",
                         "qk_done", "part_ready", "qk_ready", "kpad_in", "score_done", "max_done", "spread_ready",
                         "spread_turned", "qm_ready", "scoret_done", "exp_done", "ctx_done", "ctx_ready",
                         "ctx_turned", "cn_ready", "cn_turned", "cnt_ready", "out_done", "x_done", "chain_m",
                         "chain_c", "keys_zeroed")
                (weights_in, zeros_set, mask_ready, xn_ready, turned, z_ready, v_done, v_ready, qk_done, part_ready,
                 qk_ready, kpad_in, score_done, max_done, spread_ready, spread_turned, qm_ready, scoret_done, exp_done,
                 ctx_done, ctx_ready, ctx_turned, cn_ready, cn_turned, cnt_ready, out_done, x_done, chain_m, chain_c,
                 keys_zeroed) = (sem(n + s) for s in names)


                def over_steps(eng, step, before):
                    before()
                    for s in range(2 * GROUPS):
                        step(s, s % GROUPS, s // GROUPS % 2, s // GROUPS)
                    with eng.Fori(1, B // 2 - 1) as i:
                        for r in range(2 * GROUPS):
                            step(i * 2 * GROUPS + r, r % GROUPS, r // GROUPS, i * 2 + r // GROUPS)
                    for s in range(STEPS - 2 * GROUPS, STEPS):
                        step(s, s % GROUPS, s // GROUPS % 2, s // GROUPS)

                def known(s):
                    return isinstance(s, int)

                RING = [[(g * NU + k) % SR for k in range(NU)] for g in range(GROUPS)]
                BATCH_UNITS = GROUPS * NU

                def since(ring, g, k):
                    flat = [x for group in ring for x in group] * 2
                    at = BATCH_UNITS + g * NU + k
                    return next(d for d in range(1, BATCH_UNITS) if flat[at - d] == flat[at])

                RINGT = [[(g * NU + k) % TR for k in range(NU)] for g in range(GROUPS)]

                with nc.Block() as block:
                    @block.sync
                    def _(sp):
                        for dst, src in ((WQ, w_q), (WK, w_k), (WV, w_v), (WO, w_o), (MASKF, masks)):
                            sp.dma_start(dst[:], src).then_inc(weights_in, 16)
                        sp.wait_ge(weights_in, 80)
                        sp.wait_ge(keys_zeroed, 1)

                        def spread_keys(b, h):
                            sp.wait_ge(qk_ready, 2 * GROUPS * (b + 1))
                            for j in range(GH):
                                rows = slice(j * QR, (j + 1) * QR)
                                dst = KPAD[rows, h, :, :].bitcast(F32).rearrange("p (g j) s -> p j g s", j=GH)[:, j, :, :]
                                sp.dma_start(dst, K[rows, :, :].bitcast(F32)).then_inc(kpad_in, 16)

                        spread_keys(0, 0)
                        for b in range(1, B):
                            if b >= 2:
                                sp.wait_ge(scoret_done, (b - 1) * GROUPS * NU)
                            spread_keys(b, b % 2)
                        sp.wait_ge(kpad_in, 16 * GH * B)

                    @block.vector
                    def _(dve):
                        nc.vector.memset(V[:], 0.0).then_inc(zeros_set, 1)
                        nc.vector.memset(SPREAD[:], 0.0).then_inc(zeros_set, 1)
                        dve.wait_ge(zeros_set, 2)
                        nc.vector.memset(V[:, :, :, :, DK:DK + 1], 1.0).then_inc(zeros_set, 1)
                        dve.wait_ge(weights_in, 80)
                        nc.vector.tensor_copy(MASK[:], MASKF[:]).then_inc(mask_ready, 1)
                        ln_vector(dve)

                        def normalise(b):
                            some_wait(dve, turned, b)
                            for u in range(TPB):
                                t = b * TPB + u
                                nc.vector.tensor_scalar(XN[:, u, :], X[:, bass.ds(t, 1), :], MEAN[:, bass.ds(t, 1)],
                                                        RSTD[:, bass.ds(t, 1)], ALU.subtract,
                                                        ALU.mult).then_inc(xn_ready, 1)

                        def split(b, h, g):
                            for w, dst in enumerate((Q[:, h, g, :], K[:, g, :])):
                                at = (b * GROUPS + g) * 2 + w
                                dve.wait_ge(part_ready, at + 1)
                                if w == 0:
                                    pass
                                else:
                                    some_wait(dve, kpad_in, b * GH * 16)
                                nc.vector.tensor_tensor(dst, mixp[:], PART[:].bitcast(F32),
                                                        ALU.subtract).then_inc(qk_ready, 1)

                        def unit_max(s, g, k):
                            qt, j, m, w = QUNITS[k]
                            dve.wait_ge(score_done, s * NU + k + 1)
                            nc.vector.tensor_reduce(NMAX[:, g % 2, qt, j:j + m],
                                                    score[RING[g][k]][:, 0:m * w].rearrange("p (m w) -> p m w", m=m),
                                                    axis=AX.X, op=ALU.max, negate=True).then_inc(max_done, 1)

                        def spread_max(s, g):
                            cm = Chain(dve, chain_m, s * 2)
                            dve.wait_ge(max_done, (s + 1) * NU)
                            some_wait(dve, spread_turned, s)
                            cm.link(nc.vector.tensor_copy(NHIGH[:], NMAX[:, g % 2, :, :]))
                            columns = SPREAD[:].rearrange("p t (j r) -> p t j r", r=QR)
                            cm.link(nc.vector.tensor_copy(columns[:, :, :, MH_ROW], NHIGH[:].bitcast(F32)))
                            nc.vector.tensor_tensor(columns[:, :, :, ML_ROW], NMAX[:, g % 2, :, :],
                                                    NHIGH[:].bitcast(F32), ALU.subtract).then_inc(spread_ready, 1)

                        def add_max(s, g, h):
                            dve.wait_ge(spread_turned, s + 1)
                            some_wait(dve, scoret_done, (s - 1) * NU)
                            nc.vector.tensor_tensor(QM[:, g % 2, :], turnp[:], Q[:, h, g, :].bitcast(F32),
                                                    ALU.add).then_inc(qm_ready, 1)

                        def normalise_ctx(s, g, b):
                            cc = Chain(dve, chain_c, s)
                            dve.wait_ge(ctx_turned, s + 1)
                            ctx_v = turnp[:].rearrange("p (t j r) -> p t j r", t=TPB, r=QR)
                            cc.link(nc.vector.reciprocal(RSUM[:], ctx_v[:, :, :, DK]))
                            if g == 0:
                                some_wait(dve, cn_turned, b)
                            nc.vector.tensor_tensor(
                                CN[:].rearrange("p t (j d) -> p t j d", d=DK)[:, :, g * GH:(g + 1) * GH, :],
                                ctx_v[:, :, :, 0:DK], RSUM[:].unsqueeze(3).broadcast_to([P, TPB, GH, DK]),
                                ALU.mult).then_inc(cn_ready, 1)

                        def add_out(b):
                            dve.wait_ge(out_done, b + 1)
                            xb = X[:, bass.ds(b * TPB, TPB), :].rearrange("p t d -> p (t d)")
                            nc.vector.tensor_tensor(xb, mixp[:], xb, ALU.add).then_inc(x_done, 1)

                        def before():
                            normalise(0)
                            for g in range(GROUPS):
                                split(0, 0, g)
                            for s in range(2):
                                for k in range(NU):
                                    unit_max(s, s, k)
                                spread_max(s, s)
                                if s == 0:
                                    add_max(0, 0, 0)

                        def step(s, g, h, b):
                            more = not known(s) or s + 2 < STEPS
                            next_batch = not known(s) or b + 1 < B
                            if g == 0 and next_batch:
                                normalise(b + 1)
                            for k in range(NU):
                                if k == 3 and (not known(s) or s > 0):
                                    normalise_ctx(s - 1, (g - 1) % GROUPS, b if g > 0 else b - 1)
                                if k == 6 and (not known(s) or s + 1 < STEPS):
                                    add_max(s + 1, (g + 1) % GROUPS, h if g < 3 else 1 - h)
                                if k == 8 and g == 0 and (not known(s) or s > 0):
                                    add_out(b - 1)
                                if g < 2 and next_batch and k in (1, 5):
                                    split(b + 1, 1 - h, 2 * g + (k == 5))
                                if more:
                                    unit_max(s + 2, (g + 2) % GROUPS, k)
                            if more:
                                spread_max(s + 2, (g + 2) % GROUPS)

                        over_steps(dve, step, before)
                        normalise_ctx(STEPS - 1, GROUPS - 1, B - 1)
                        add_out(B - 1)
                        dve.wait_ge(x_done, B)

                    @block.scalar
                    def _(act):
                        nc.scalar.preload_act_table_set(LN_EXP)
                        ln_scalar(act)
                        act.wait_ge(zeros_set, 3)

                        def values(b, h):
                            act.wait_ge(turned, b + 1)
                            some_wait(act, qk_done, 2 * GROUPS * b)
                            nc.scalar.activation(Z[:], turnp[:], ACT.Copy).then_inc(z_ready, 1)
                            act.wait_ge(v_done, b + 1)
                            some_wait(act, ctx_done, (b - 1) * GROUPS)
                            nc.scalar.activation(
                                V[:, h, :, :, 0:DK], mixp[:].rearrange("p (t a d) -> p t a d", t=TPB, d=DK),
                                ACT.Copy).then_inc(v_ready, 1)

                        def parts(b, h, g):
                            for w in range(2):
                                at = (b * GROUPS + g) * 2 + w
                                act.wait_ge(qk_done, at + 1)
                                some_wait(act, qk_ready, at)
                                pick = CT[:, CONST["pick_q" if w == 0 else "pick_k"]]
                                if w == 0:
                                    nc.scalar.activation(PART[:], mixp[:], ACT.Identity,
                                                         scale=pick).then_inc(part_ready, 1)
                                else:
                                    nc.scalar.activation(PART[:], mixp[:], ACT.Identity, scale=pick,
                                                         bias=CT[:, CONST["bias_k"]]).then_inc(part_ready, 1)

                        def unit_exp(s, g, k):
                            kb, j, m, w = KUNITS[k]
                            act.wait_ge(scoret_done, s * NU + k + 1)
                            if k == 0:
                                some_wait(act, ctx_done, s - 1)
                            nc.scalar.activation(PT[:, g % 2, j:j + m, KOFF[kb]:KOFF[kb] + w],
                                                 scoret[RINGT[g][k]][:, 0:m * w].rearrange("p (m w) -> p m w", m=m),
                                                 ACT.Exp, scale=SCALE).then_inc(exp_done, 1)

                        def ctx_copy(s):
                            act.wait_ge(ctx_done, s + 1)
                            some_wait(act, ctx_turned, s)
                            nc.scalar.activation(CTX[:], ctxp[:], ACT.Copy).then_inc(ctx_ready, 1)

                        def cn_copy(b):
                            act.wait_ge(cn_turned, b + 1)
                            some_wait(act, out_done, b)
                            nc.scalar.activation(CNT[:], turnp[:], ACT.Copy).then_inc(cnt_ready, 1)

                        def before():
                            values(0, 0)
                            for g in range(GROUPS):
                                parts(0, 0, g)

                        def step(s, g, h, b):
                            next_batch = not known(s) or b + 1 < B
                            for k in range(NU):
                                if k == 0 and g == 0 and next_batch:
                                    values(b + 1, 1 - h)
                                if g < 2 and next_batch and k in (1, 5):
                                    parts(b + 1, 1 - h, 2 * g + (k == 5))
                                unit_exp(s, g, k)
                                if k == 1 and (not known(s) or s > 0):
                                    ctx_copy(s - 1)
                                if k == 6 and g == 0 and (not known(s) or s > 0):
                                    cn_copy(b - 1)

                        over_steps(act, step, before)
                        ctx_copy(STEPS - 1)
                        cn_copy(B - 1)

                    @block.gpsimd
                    def _(pool):
                        nc.gpsimd.memset(KPAD[:].bitcast(F32), 0.0).then_inc(keys_zeroed, 1)

                    @block.tensor
                    def _(pe):
                        pe.wait_ge(weights_in, 80)
                        pe.wait_ge(mask_ready, 1)
                        pe.wait_ge(keys_zeroed, 1)
                        pe.wait_ge(zeros_set, 3)

                        def values(b, h):
                            pe.wait_ge(xn_ready, (b + 1) * TPB)
                            some_wait(pe, qk_ready, 2 * GROUPS * b)
                            for u in range(TPB):
                                last = nc.tensor.transpose(turnp[:, u * P:(u + 1) * P], XN[:, u, :], IDENT)
                            last.then_inc(turned, 1)
                            pe.wait_ge(z_ready, b + 1)
                            for u in range(TPB):
                                last = nc.tensor.matmul(mixp[:, u * P:(u + 1) * P], Z[:, u * P:(u + 1) * P], WV[:],
                                                        start=True, stop=True)
                            last.then_inc(v_done, 1)

                        def project(b, g):
                            for w, weight in enumerate((WQ, WK)):
                                at = (b * GROUPS + g) * 2 + w
                                if g == 0 and w == 0:
                                    pe.wait_ge(v_ready, b + 1)
                                if g == 2 and w == 0:
                                    some_wait(pe, x_done, b - 1)
                                some_wait(pe, qk_ready, at)
                                nc.tensor.matmul(mixp[:], weight[:, g, :], Z[:], start=True,
                                                 stop=True).then_inc(qk_done, 1)

                        def unit_score(s, g, h, k):
                            qt, j, m, w = QUNITS[k]
                            bank = score[RING[g][k]]
                            some_wait(pe, max_done, s * NU + k + 1 - since(RING, g, k))
                            for a in range(m):
                                nc.tensor.matmul(bank[:, a * w:(a + 1) * w], Q[:, h, g, qt * P:(qt + 1) * P],
                                                 KPAD[:, h, g * GH + j + a, 0:w], start=True, stop=False)
                                last = nc.tensor.matmul(bank[:, (a + 1) * w - P:(a + 1) * w], MASK[:, 0, :],
                                                        MASK[:, 1, :], start=False, stop=True)
                            last.then_inc(score_done, 1)

                        def turn_max(s):
                            pe.wait_ge(spread_ready, s + 1)
                            some_wait(pe, cn_ready, s - 1)
                            for u in range(TPB):
                                last = nc.tensor.transpose(turnp[:, u * P:(u + 1) * P], SPREAD[:, u, :], IDENT)
                            last.then_inc(spread_turned, 1)

                        def unit_scoret(s, g, h, k):
                            kb, j, m, w = KUNITS[k]
                            bank = scoret[RINGT[g][k]]
                            some_wait(pe, exp_done, s * NU + k + 1 - since(RINGT, g, k))
                            for a in range(m):
                                nc.tensor.matmul(bank[:, a * w:(a + 1) * w], KPAD[:, h, g * GH + j + a, kb * P:(kb + 1) * P],
                                                 QM[:, g % 2, kb * P:S], start=True, stop=False)
                                last = nc.tensor.matmul(bank[:, a * w:a * w + P], MASK[:, 0, :], MASK[:, 2, :],
                                                        start=False, stop=True)
                            last.then_inc(scoret_done, 1)

                        def weigh(s, g, h, kb):
                            need = {0: 4, 1: 8, 2: 10, 3: 11}[kb]
                            pe.wait_ge(exp_done, s * NU + need)
                            if kb == 0:
                                some_wait(pe, ctx_ready, s)
                            for j in range(GH):
                                last = nc.tensor.matmul(ctxp[j * QR:(j + 1) * QR, kb * P:S], V[:, h, kb, g * GH + j, :],
                                                        PT[:, g % 2, j, KOFF[kb]:KOFF[kb] + S - kb * P],
                                                        start=(kb == 0), stop=(kb == TPB - 1),
                                                        tile_position=(0, j * QR))
                            if kb == TPB - 1:
                                last.then_inc(ctx_done, 1)

                        def turn_ctx(s):
                            pe.wait_ge(ctx_ready, s + 1)
                            some_wait(pe, cn_ready, s)
                            for u in range(TPB):
                                last = nc.tensor.transpose(turnp[:, u * P:(u + 1) * P], CTX[:, u * P:(u + 1) * P], IDENT)
                            last.then_inc(ctx_turned, 1)

                        def turn_cn(b):
                            pe.wait_ge(cn_ready, (b + 1) * GROUPS)
                            if not known(b) or b + 1 < B:
                                pe.wait_ge(qm_ready, (b + 1) * GROUPS + 2)
                            for u in range(TPB):
                                last = nc.tensor.transpose(turnp[:, u * P:(u + 1) * P], CN[:, u, :], IDENT)
                            last.then_inc(cn_turned, 1)

                        def project_out(b):
                            pe.wait_ge(cnt_ready, b + 1)
                            some_wait(pe, x_done, b)
                            if known(b) and b + 2 >= B:
                                pe.wait_ge(qk_ready, 2 * GROUPS * B)
                            else:
                                pe.wait_ge(qk_ready, 2 * GROUPS * (b + 2) + 4)
                            for u in range(TPB):
                                last = nc.tensor.matmul(mixp[:, u * P:(u + 1) * P], CNT[:, u * P:(u + 1) * P], WO[:],
                                                        start=True, stop=True)
                            last.then_inc(out_done, 1)

                        def before():
                            values(0, 0)
                            for g in range(GROUPS):
                                project(0, g)
                            pe.wait_ge(qk_ready, 2 * GROUPS)
                            pe.wait_ge(kpad_in, 16 * GH)
                            for s in range(2):
                                for k in range(NU):
                                    unit_score(s, s, 0, k)
                                if s == 0:
                                    turn_max(0)

                        def step(s, g, h, b):
                            prev = not known(s) or s > 0
                            more = not known(s) or s + 2 < STEPS
                            next_batch = not known(s) or b + 1 < B
                            hn = h if g < 2 else 1 - h
                            pe.wait_ge(qm_ready, s + 1)
                            if g == 2 and more:
                                pe.wait_ge(kpad_in, 16 * GH * (b + 2))
                                pe.wait_ge(qk_ready, 2 * GROUPS * (b + 2))
                            for k in range(NU):
                                if k == 0 and g == 0 and next_batch:
                                    values(b + 1, 1 - h)
                                if g < 2 and next_batch and k in (1, 5):
                                    project(b + 1, 2 * g + (k == 5))
                                unit_scoret(s, g, h, k)
                                if k == 0 and prev:
                                    hp = h if g > 0 else 1 - h
                                    weigh(s - 1, (g - 1) % GROUPS, hp, 2)
                                    weigh(s - 1, (g - 1) % GROUPS, hp, 3)
                                if k == 2 and prev:
                                    turn_ctx(s - 1)
                                if k == 5 and (not known(s) or s + 1 < STEPS):
                                    turn_max(s + 1)
                                if k == 6:
                                    weigh(s, g, h, 0)
                                if k == 7 and g == 0 and prev:
                                    turn_cn(b - 1)
                                if k == 8 and g == 0 and prev:
                                    project_out(b - 1)
                                if more:
                                    unit_score(s + 2, (g + 2) % GROUPS, hn, k)
                                if k == NU - 1:
                                    weigh(s, g, h, 1)

                        over_steps(pe, step, before)
                        weigh(STEPS - 1, GROUPS - 1, 1, 2)
                        weigh(STEPS - 1, GROUPS - 1, 1, 3)
                        turn_ctx(STEPS - 1)
                        turn_cn(B - 1)
                        project_out(B - 1)

        def store():
            stored = sem("stored")
            with nc.Block() as block:
                @block.sync
                def _(sp):
                    sp.dma_start(out_tok, X[:]).then_inc(stored, 16)
                    sp.wait_ge(stored, 16)

        with ExitStack() as experts_ctx:
            W1, W3 = (sb(name, [P, E, FF], F32, experts_ctx) for name in ("W1", "W3"))
            W2 = sb("W2", [P, E, FC, D], F32, experts_ctx)
            GW = sb("GW", [P, E], F32, experts_ctx)
            experts(0)
            scan_layer()
            experts(1)
        nc.clear_and_free_semaphores(nc.allocated_since(no_semaphores))
        nc.all_engine_barrier()
        shifted_ffn(0)
        attention()
        shifted_ffn(1)
        store()


def lay_out(d):
    f = lambda a: np.ascontiguousarray(np.asarray(a))
    i = np.arange(P)
    vecs = np.zeros((P, 8 + KC), np.float32)
    for v, name in enumerate(("L0_attn_norm_scale", "L0_attn_conv_b", "L0_attn_dt_bias", "L1_ffn_mu_r", "L1_ffn_mu_k")):
        vecs[:, v] = f(d[name])
    conv_diag = np.zeros((P, KC, P), np.float32)
    for w in range(KC):
        conv_diag[i, w, i] = f(d["L0_attn_conv_w"])[:, 0, w]
    w = f(d["L0_attn_in_proj_w"])
    v = w[:, D:2 * D]
    swapped = v.reshape(D, HM, 2, DH // 2)[:, :, ::-1, :].reshape(D, D)
    in_proj = f(np.stack([w[:, 0:D], w[:, 2 * D:3 * D], v, swapped], 1))
    head_mix = np.zeros((P, P), np.float32)
    for r in range(DH):
        head_mix[np.ix_(np.arange(HM) * DH + r, np.arange(HM) * DH + r)] = f(d["L0_attn_head_mix"])
    ffn_w = f(np.stack([f(d["L1_ffn_W_r"]).T, f(d["L1_ffn_W_k"]).T, f(d["L1_ffn_W_v"]).T], 1))
    qkv = f(d["L1_attn_W_qkv"])
    qk = np.zeros((2, P, GROUPS, P), np.float32)
    for w in range(2):
        for h in range(HA):
            for part in range(3):
                at = QR * (h % GH) + DK * part
                qk[w, :, h // GH, at:at + DK] = qkv[w, h].T
    masks = np.zeros((P, 3, P), np.float32)
    masks[:, 0] = np.eye(P)
    masks[:, 1] = np.where(i[None, :] > i[:, None], NEG, 0)
    masks[:, 2] = np.where(i[:, None] > i[None, :], NEG, 0)
    return dict(x=f(d["L0_attn_x"]).reshape(T, D), consts=constant_table(), gate_w=f(d["L0_ffn_gate_w"]),
                w1=f(d["L0_ffn_w1"]), w3=f(d["L0_ffn_w3"]), w2=f(d["L0_ffn_w2"]), vecs=vecs, conv_diag=conv_diag,
                in_proj=in_proj, head_mix=head_mix, out_proj=f(d["L0_attn_out_proj_w"]), ffn_w=ffn_w,
                w_q=qk[0], w_k=qk[1], w_v=f(qkv[2].reshape(D, D).T), w_o=f(f(d["L1_attn_W_o"]).T), masks=masks)


def kernel(**inputs):
    import concourse.bacc as _bacc
    from concourse.bass_utils import run_bass_kernel_spmd as _run

    nc = _bacc.Bacc("TRN2", target_bir_lowering=False, num_devices=1)
    arrays, args = {}, {}
    for name, a in lay_out(inputs).items():
        arrays[f"in_{name}_dram"] = a
        args[name] = nc.dram_tensor(f"in_{name}_dram", a.shape, mybir.dt.from_np(a.dtype), kind="ExternalInput").ap()
    out = nc.dram_tensor("out_0_dram", (T, D), F32, kind="ExternalOutput").ap()
    build_macaron(nc, out=out, **args)
    r = _run(nc, [arrays], core_ids=[0])
    return r.results[0]["out_0_dram"].reshape(B, S, D)
```

```python
import math
from contextlib import ExitStack

import numpy as np

import concourse.bass as bass
from concourse import mybir

F32 = mybir.dt.float32
F32R = mybir.dt.float32r
BF16 = mybir.dt.bfloat16
I32 = mybir.dt.int32
U32 = mybir.dt.uint32
ALU = mybir.AluOpType
ACT = mybir.ActivationFunctionType
AX = mybir.AxisListType
LN_EXP = "natural_log_exp_and_others"

P = 128
B, S, D = 8, 512, 128
T = B * S
TILES = T // P
TPB = S // P
E, FF = 8, 512
FC = FF // P
SLOT_TILES = (2 * T) // P + E
EPS_LN, EPS_RMS = 1e-5, 1e-6
HM = 16
DH = D // HM
KC = 4
CHUNK = 32
CHUNKS = S // CHUNK
ROPE_BASE = 10000.0
HA = 16
DK = D // HA
GH = 4
GROUPS = HA // GH
QR = P // GH
MH_ROW, ML_ROW = 3 * DK, 3 * DK + 1
NEG = -1e30

CONST = {}
_at = 0
for _name, _width in (("bias_k", 1), ("pick_q", 1), ("pick_k", 1), ("ident", P), ("before", P), ("ones", P), ("rev", TILES * E), ("newexp", E * TILES),
                      ("tile0", SLOT_TILES), ("partition", 1), ("iota", P), ("tileno", TILES), ("cos", S), ("sin", S), ("newchunk", S)):
    CONST[_name] = slice(_at, _at + _width)
    _at += _width
CONST_COLS = _at
SCAN_TABLES = CONST["cos"].start


def constant_table():
    c = np.zeros((P, CONST_COLS), np.float32)
    p = np.arange(P)
    c[:, CONST["ident"]] = np.eye(P)
    c[:, CONST["before"]] = p[:, None] < p[None, :]
    c[:, CONST["ones"]] = 1.0
    c[:, CONST["rev"]] = np.tile(E - np.arange(E), TILES)
    newexp = np.ones((E, TILES))
    newexp[:, 0] = 0
    c[:, CONST["newexp"]] = newexp.ravel()
    c[:, CONST["tile0"]] = P * np.arange(SLOT_TILES)
    c[:, CONST["partition"]] = p[:, None]
    c[:, CONST["iota"]] = p
    c[:, CONST["tileno"]] = np.arange(TILES)
    row = p % QR
    c[:, CONST["pick_q"]] = ((row >= 2 * DK) & (row < 3 * DK))[:, None]
    c[:, CONST["pick_k"]] = ((row >= DK) & (row < 2 * DK))[:, None]
    c[:, CONST["bias_k"]] = -1.0 * ((row == MH_ROW) | (row == ML_ROW))[:, None]
    freq = (np.float32(1.0) / np.float32(ROPE_BASE) ** (np.arange(0, DH, 2, dtype=np.float32) / np.float32(DH)))
    angle = np.arange(S, dtype=np.float32)[None, :] * freq.astype(np.float32)[(p % DH) % (DH // 2)][:, None]
    c[:, CONST["cos"]] = np.cos(angle)
    c[:, CONST["sin"]] = np.sin(angle) * np.where(p % DH < DH // 2, -1.0, 1.0)[:, None]
    c[:, CONST["newchunk"]] = (np.arange(S) % CHUNK != 0)
    return c


class Chain:

    def __init__(self, eng, sem, start=0):
        self.eng, self.sem, self.start, self.n = eng, sem, start, 0

    def link(self, ins):
        ins.then_inc(self.sem, 1)
        self.n += 1
        self.eng.wait_ge(self.sem, self.start + self.n)


class Norm:

    def __init__(self, mean, rstd, minus, roots, ready, stats, guess, finish):
        self.mean, self.rstd, self.minus, self.roots = mean, rstd, minus, roots
        self.ready, self.stats, self.guess, self.finish = ready, stats, guess, finish


def build_macaron(nc, x, consts, gate_w, w1, w3, w2, vecs, conv_diag, in_proj, head_mix, out_proj, ffn_w, w_q, w_k, w_v, w_o, masks, out):
    with ExitStack() as ctx:
        sb = lambda name, shape, dt=F32, c=ctx: c.enter_context(nc.sbuf_tensor(name, shape, dt))
        ps = lambda name, shape, dt=F32, c=ctx: c.enter_context(nc.psum_tensor(name, shape, dt))
        sem = nc.alloc_semaphore
        no_semaphores = nc.snapshot_sems()

        X = sb("X", [P, TILES, D])
        SLOT = [sb(f"SLOT{j}", [P, TILES], U32) for j in range(2)]
        WT = [sb(f"WT{j}", [P, TILES]) for j in range(2)]
        CT = sb("CT", [P, CONST_COLS])
        IOTA, TILENO = CT[:, CONST["iota"]], CT[:, CONST["tileno"]]
        IDENT, BEFORE, ONES = CT[:, CONST["ident"]], CT[:, CONST["before"]], CT[:, CONST["ones"]]
        XS = nc.dram_tensor("xs_scratch", (T, D), F32).ap()
        YS = nc.dram_tensor("ys_scratch", (SLOT_TILES * P, D), F32).ap()
        x_tok = x.rearrange("(t p) d -> p t d", p=P)
        out_tok = out.rearrange("(t p) d -> p t d", p=P)

        VEC = sb("VEC", [P, 8 + KC])
        NORM_SCALE, CONV_B, DT_BIAS, MU_R, MU_K = (VEC[:, v:v + 1] for v in range(5))

        def some_wait(eng, s, v):
            if not isinstance(v, int) or v > 0:
                eng.wait_ge(s, v)

        def over_batches(eng, body, unroll=False):
            body(None, 0, None, 0)
            body(None, 1, 0, 1)
            body(0, 0, 1, 2)
            body(1, 1, 2, 3)
            if unroll:
                for b in range(2, B - 2):
                    body(b, b % 2, b + 1, b + 2)
            else:
                with eng.Fori(1, B // 2 - 1) as i:
                    for h in range(2):
                        b = i * 2 + h
                        body(b, h, b + 1, b + 2)
            body(B - 2, 0, B - 1, None)
            body(B - 1, 1, None, None)

        def layernorm(name, c, tiles=TPB, halves=2, roots=1, tables=False):
            ST = sb(name + "_ST", [P, halves, tiles, 6], F32, c)
            MEAN, VAR, A0, A1, SUM, LESS = (sb(f"{name}_m{k}", [P, halves, tiles], F32, c) for k in range(6))
            VE, ROOT, SQ, HALF = (sb(f"{name}_v{k}", [P, halves, roots, tiles], F32, c) for k in range(4))
            stats_done, link_sem = sem(name + "_stats_done"), sem(name + "_link")
            ln_ready = sem(name + "_ready")
            MR = sb(name + "_mr", [P, halves, tiles], F32, c)
            LINKS = 5 + 4 if tables else 6 + 3 * 4
            if tables:
                ve_ready, ln_done, guessed = (sem(f"{name}_{s}") for s in ("ve_ready", "ln_done", "guessed"))

            def guess(act, b, h):
                act.wait_ge(ve_ready, b + 1)
                nc.scalar.activation(SQ[:, h], VE[:, h], ACT.Ln).then_inc(ln_done, 1)
                act.wait_ge(ln_done, b + 1)
                nc.scalar.activation(ROOT[:, h], SQ[:, h], ACT.Exp, scale=-0.5).then_inc(guessed, 1)

            def stats(dve, b, h, x_tile):
                for u in range(tiles):
                    nc.vector.bn_stats(ST[:, h, u, :], x_tile(u)).then_inc(stats_done, 1)

            def finish(eng, run, b, h):
                eng.wait_ge(stats_done, tiles * (b + 1))
                ch = Chain(eng, link_sem, b * LINKS)
                st, total, mean, less, var, a0, a1 = ST[:, h], SUM[:, h], MEAN[:, h], LESS[:, h], VAR[:, h], A0[:, h], A1[:, h]
                ve, half, root, sq = VE[:, h], HALF[:, h], ROOT[:, h], SQ[:, h]
                run.tensor_tensor(a0, st[:, :, 2], st[:, :, 5], ALU.add)
                run.tensor_tensor(total, st[:, :, 1], st[:, :, 4], ALU.add)
                ch.link(run.tensor_tensor(a1, st[:, :, 1], st[:, :, 4], ALU.subtract))
                run.tensor_scalar(mean, total, 0.5, None, ALU.mult)
                run.tensor_scalar(less, total, -0.5, None, ALU.mult)
                run.tensor_scalar(a0, a0, 1.0 / D, None, ALU.mult)
                ch.link(run.tensor_scalar(a1, a1, 0.5, None, ALU.mult))
                ch.link(run.tensor_tensor(a1, a1, a1, ALU.mult))
                ch.link(run.tensor_tensor(var, a1, a0, ALU.add))
                if roots == 2:
                    run.tensor_scalar(ve[:, 1, :], var, 1.0 + EPS_RMS, EPS_RMS * EPS_LN, ALU.mult, ALU.add)
                ch.link(run.tensor_scalar(ve[:, 0, :], var, EPS_LN, None, ALU.add))
                if tables:
                    eng.sem_inc(ve_ready, 1)
                    run.tensor_scalar(half, ve, -0.5, None, ALU.mult)
                    eng.wait_ge(guessed, b + 1)
                else:
                    run.tensor_scalar(half, ve, -0.5, None, ALU.mult)
                    ch.link(run.tensor_scalar(root.bitcast(I32), ve.bitcast(I32), -0.5, float(0x5F3759DF), ALU.mult,
                                              ALU.add))
                for _ in range(1 if tables else 3):
                    ch.link(run.tensor_tensor(sq, root, root, ALU.mult))
                    ch.link(run.tensor_tensor(sq, sq, half, ALU.mult))
                    ch.link(run.tensor_scalar(sq, sq, 1.5, None, ALU.add))
                    ch.link(run.tensor_tensor(root, sq, root, ALU.mult))
                run.tensor_tensor(MR[:, h], less, root[:, 0, :], ALU.mult).then_inc(ln_ready, 1)
                assert ch.n == LINKS

            return Norm(mean=lambda h, u: MEAN[:, h, u:u + 1], rstd=lambda h, u, r=0: ROOT[:, h, r, u:u + 1],
                        minus=lambda h, u: MR[:, h, u:u + 1], roots=ROOT, ready=ln_ready, stats=stats, guess=guess, finish=finish)

        def experts(k):
            n = f"m{k}_"
            with ExitStack() as inner:
                loaded = {s: sem(f"{n}{s}_loaded") for s in ("x", "table", "gate", "w1", "w3", "w2", "rest")} if k == 0 else None
                EID = sb(n + "EID", [1, SLOT_TILES], I32, inner)
                TOKEN = sb(n + "TOKEN", [P, SLOT_TILES], U32, inner)
                t8 = lambda s: sb(n + s, [P, TILES, E], F32, inner)
                AL, NUM, PR = t8("AL"), [t8("NUM1"), t8("NUM2")], [t8("P1"), t8("P2")]
                M = [sb(f"{n}M{j}", [P, TILES], F32, inner) for j in range(2)]
                exp_done = sem(n + "exp_done")
                route(k, n, loaded, EID, TOKEN, AL, NUM, PR, M, exp_done)
                run_experts(n, EID, TOKEN, AL, NUM, PR, M)

        def route(k, n, loaded, EID, TOKEN, AL, NUM, PR, M, exp_done):
            with ExitStack() as c:
                ln = layernorm(n + "ln", c, tiles=TILES, halves=1)
                XN = sb(n + "XN", [P, TILES, D], F32, c)
                XT = sb(n + "XT", [P, 2, S], F32, c)
                t8 = lambda s: sb(n + s, [P, TILES, E], F32, c)
                L, L2, Q, ONE1, ONE2, POS = (t8(s) for s in ("L", "L2", "Q", "ONE1", "ONE2", "POS"))
                QM = sb(n + "QM", [P, TILES], F32, c)
                TOT = sb(n + "TOT", [P, E, TILES], F32, c)
                INCL = sb(n + "INCL", [P, E, TILES], F32, c)
                PADI = sb(n + "PADI", [P, E], I32, c)
                PAD = sb(n + "PAD", [P, E], F32, c)
                END = sb(n + "END", [P, E], F32, c)
                BASE = sb(n + "BASE", [P, E], F32, c)
                CMP = sb(n + "CMP", [1, SLOT_TILES, E], F32, c)
                EF = sb(n + "EF", [1, SLOT_TILES], F32, c)
                SLOTF = sb(n + "SLOTF", [P, TILES, 2], F32, c)
                SLOTI, HIGH, LOW = (sb(n + s, [P, TILES, 2], I32, c) for s in ("SLOTI", "HIGH", "LOW"))
                HIGHB, LOWB = (sb(n + s, [P, TILES, 2], BF16, c) for s in ("HIGHB", "LOWB"))
                TILE1 = sb(n + "TILE1", [P, TILES, 2, SLOT_TILES], BF16, c)
                TILEX = sb(n + "TILEX", [P, TILES, 2, 2, SLOT_TILES], BF16, c)
                ROW1 = sb(n + "ROW1", [P, TILES, 2, P], BF16, c)
                TOKENF = sb(n + "TOKENF", [P, SLOT_TILES], F32, c)
                TP = [ps(f"{n}TP{h}", [P, S], F32, c) for h in range(2)]
                LG = ps(n + "LG", [P, TILES, E], F32, c)
                RK = ps(n + "RK", [P, 2, TILES, E], F32, c)
                INV = ps(n + "INV", [P, 2, SLOT_TILES], F32, c)
                (xn_ready, turned, xt_ready, logits_done, num_ready, choice_ready, ranks_done, route_link, tiles_ready,
                 rows_ready, inverse_done, xn_stored) = (sem(n + s) for s in (
                    "xn_ready", "turned", "xt_ready", "logits_done", "num_ready", "choice_ready", "ranks_done",
                    "route_link", "tiles_ready", "rows_ready", "inverse_done", "xn_stored"))
                tile_t = sem(n + "tile_t")
                if k == 0:
                    w_high = sem(n + "w_high")
                wide = lambda v: v.unsqueeze(2).broadcast_to([P, TILES, E])
                REV = CT[:, CONST["rev"]].rearrange("p (t e) -> p t e", e=E)
                PIECES = 4
                TPP = TILES // PIECES

                with nc.Block() as block:
                    @block.sync
                    def _(sp):
                        if k == 0:
                            sp.dma_start(X[:], x_tok).then_inc(loaded["x"], 16)
                            sp.dma_start(CT[:, 0:SCAN_TABLES], consts[:, 0:SCAN_TABLES]).then_inc(loaded["table"], 16)
                            sp.dma_start(GW[:], gate_w).then_inc(loaded["gate"], 16)
                            sp.dma_start(W1[:], w1.rearrange("e p f -> p e f")).then_inc(loaded["w1"], 16)
                            sp.dma_start(W3[:], w3.rearrange("e p f -> p e f")).then_inc(loaded["w3"], 16)
                        for b in range(B):
                            sp.wait_ge(xn_ready, (b + 1) * TPB)
                            sp.dma_start(XS.rearrange("(t p) d -> p t d", p=P)[:, b * TPB:(b + 1) * TPB, :],
                                         XN[:, b * TPB:(b + 1) * TPB, :]).then_inc(xn_stored, 16)
                        if k == 0:
                            sp.dma_start(W2[:], w2.rearrange("e (c p) d -> p e c d", p=P)).then_inc(loaded["w2"], 16)
                            sp.dma_start(CT[:, SCAN_TABLES:], consts[:, SCAN_TABLES:]).then_inc(loaded["rest"], 16)
                            sp.dma_start(VEC[:], vecs).then_inc(loaded["rest"], 16)
                            sp.wait_ge(loaded["w2"], 16)
                            sp.wait_ge(loaded["rest"], 32)
                        sp.wait_ge(xn_stored, 16 * B)

                    @block.vector
                    def _(dve):
                        if k == 0:
                            dve.wait_ge(loaded["x"], 16)
                        ln.stats(dve, 0, 0, lambda u: X[:, u, :])
                        ln.finish(dve, nc.vector, 0, 0)
                        for t in range(TILES):
                            nc.vector.tensor_scalar(XN[:, t, :], X[:, t, :], ln.mean(0, t), ln.rstd(0, t), ALU.subtract,
                                                    ALU.mult).then_inc(xn_ready, 1)
                        ch = Chain(dve, route_link)
                        if k == 0:
                            dve.wait_ge(loaded["table"], 16)
                        dve.wait_ge(logits_done, B)
                        ch.link(nc.vector.tensor_copy(L[:], LG[:]))
                        ch.link(nc.vector.tensor_reduce(M[0][:], L[:], axis=AX.X, op=ALU.max))

                        def first_of(dst, src, m):
                            ch.link(nc.vector.tensor_tensor(Q[:], src[:], wide(m[:]), ALU.is_equal))
                            ch.link(nc.vector.tensor_tensor(Q[:], Q[:], REV, ALU.mult))
                            ch.link(nc.vector.tensor_reduce(QM[:], Q[:], axis=AX.X, op=ALU.max))
                            ch.link(nc.vector.tensor_tensor(dst[:], Q[:], wide(QM[:]), ALU.is_equal))

                        first_of(ONE1, L, M[0])
                        ch.link(nc.vector.scalar_tensor_tensor(out=L2[:], in0=ONE1[:], scalar=-1e38, in1=L[:],
                                                               op0=ALU.mult, op1=ALU.add))
                        ch.link(nc.vector.tensor_reduce(M[1][:], L2[:], axis=AX.X, op=ALU.max))
                        first_of(ONE2, L2, M[1])
                        nc.vector.tensor_tensor(Q[:], ONE1[:], ONE2[:], ALU.add).then_inc(choice_ready, 1)
                        nc.vector.tensor_tensor(NUM[0][:], wide(M[0][:]), L[:], ALU.subtract).then_inc(num_ready, 1)
                        nc.vector.tensor_tensor(NUM[1][:], wide(M[1][:]), L2[:], ALU.subtract).then_inc(num_ready, 1)
                        nc.vector.scalar_tensor_tensor(out=AL[:], in0=L[:], scalar=-1.0, in1=L[:], op0=ALU.mult,
                                                       op1=ALU.max)
                        dve.wait_ge(ranks_done, 1)
                        ch.link(nc.vector.tensor_copy(TOT[:].rearrange("p e t -> p t e"), RK[:, 1, :, :]))
                        ch.link(nc.vector.tensor_tensor_scan(out=INCL[:].rearrange("p e t -> p (e t)"),
                                                             data0=CT[:, CONST["newexp"]],
                                                             data1=TOT[:].rearrange("p e t -> p (e t)"), initial=0.0,
                                                             op0=ALU.mult, op1=ALU.add))
                        ch.link(nc.vector.tensor_scalar(PADI[:], INCL[:, :, TILES - 1], float(P - 1), None, ALU.add))
                        ch.link(nc.vector.tensor_scalar(PADI[:], PADI[:], -P, None, ALU.bitwise_and))
                        ch.link(nc.vector.tensor_copy(PAD[:], PADI[:]))
                        ch.link(nc.vector.tensor_tensor_scan(out=END[:], data0=CT[:, CONST["ones"]][:, 0:E],
                                                             data1=PAD[:], initial=0.0, op0=ALU.mult, op1=ALU.add))
                        nc.vector.tensor_tensor(BASE[:], END[:], PAD[:], ALU.subtract)
                        ch.link(nc.vector.tensor_tensor(INCL[:], INCL[:], TOT[:], ALU.subtract))
                        ch.link(nc.vector.tensor_tensor(INCL[:], INCL[:],
                                                        BASE[:].unsqueeze(2).broadcast_to([P, E, TILES]), ALU.add))
                        ch.link(nc.vector.tensor_tensor(POS[:], INCL[:].rearrange("p e t -> p t e"), RK[:, 0, :, :],
                                                        ALU.add))
                        nc.vector.tensor_tensor(ONE1[:], ONE1[:], POS[:], ALU.mult)
                        ch.link(nc.vector.tensor_tensor(ONE2[:], ONE2[:], POS[:], ALU.mult))
                        nc.vector.tensor_reduce(SLOTF[:, :, 0], ONE1[:], axis=AX.X, op=ALU.add)
                        ch.link(nc.vector.tensor_reduce(SLOTF[:, :, 1], ONE2[:], axis=AX.X, op=ALU.add))
                        ch.link(nc.vector.tensor_copy(SLOTI[:], SLOTF[:]))
                        nc.vector.tensor_scalar(HIGH[:], SLOTI[:], 7, None, ALU.arith_shift_right)
                        ch.link(nc.vector.tensor_scalar(LOW[:], SLOTI[:], P - 1, None, ALU.bitwise_and))
                        nc.vector.tensor_copy(HIGHB[:], HIGH[:])
                        ch.link(nc.vector.tensor_copy(LOWB[:], LOW[:]))
                        ch.link(nc.vector.tensor_tensor(
                            TILE1[:], HIGHB[:].unsqueeze(3).broadcast_to([P, TILES, 2, SLOT_TILES]),
                            IOTA[:, 0:SLOT_TILES].unsqueeze(1).unsqueeze(1).broadcast_to([P, TILES, 2, SLOT_TILES]),
                            ALU.is_equal))
                        dve.sem_inc(tiles_ready, 1)
                        ch.link(nc.vector.tensor_scalar(TILEX[:, :, :, 0, :], TILE1[:], CT[:, CONST["partition"]], None,
                                                        ALU.mult))
                        for q in range(PIECES):
                            some = slice(q * TPP, (q + 1) * TPP)
                            nc.vector.tensor_tensor(
                                ROW1[:, some], LOWB[:, some].unsqueeze(3).broadcast_to([P, TPP, 2, P]),
                                IOTA[:].unsqueeze(1).unsqueeze(1).broadcast_to([P, TPP, 2, P]),
                                ALU.is_equal).then_inc(rows_ready, 1)
                        nc.vector.tensor_copy(SLOT[0][:], SLOTF[:, :, 0])
                        nc.vector.tensor_copy(SLOT[1][:], SLOTF[:, :, 1])
                        ch.link(nc.vector.tensor_tensor(CMP[:],
                                                        END[0:1, :].unsqueeze(1).broadcast_to([1, SLOT_TILES, E]),
                                                        CT[0:1, CONST["tile0"]].unsqueeze(2)
                                                        .broadcast_to([1, SLOT_TILES, E]), ALU.is_le))
                        ch.link(nc.vector.tensor_reduce(EF[:], CMP[:], axis=AX.X, op=ALU.add))
                        ch.link(nc.vector.tensor_scalar(EID[:], EF[:], float(E - 1), None, ALU.min))
                        dve.wait_ge(inverse_done, 1)
                        ch.link(nc.vector.tensor_copy(TOKENF[:], INV[:, 0, :]))
                        ch.link(nc.vector.scalar_tensor_tensor(out=TOKENF[:], in0=INV[:, 1, :], scalar=float(P),
                                                               in1=TOKENF[:], op0=ALU.mult, op1=ALU.add))
                        ch.link(nc.vector.tensor_copy(TOKEN[:], TOKENF[:]))

                    @block.scalar
                    def _(act):
                        nc.scalar.preload_act_table(ACT.Exp)
                        for b in range(B):
                            act.wait_ge(turned, b + 1)
                            some_wait(act, logits_done, b - 1)
                            nc.scalar.activation(XT[:, b % 2, :], TP[b % 2][:], ACT.Copy).then_inc(xt_ready, 1)
                        if k == 0:
                            act.wait_ge(loaded["w1"], 16)
                            nc.scalar.activation(W1H[:], W1[:], ACT.Copy).then_inc(w_high, 1)
                            act.wait_ge(loaded["w3"], 16)
                            nc.scalar.activation(W3H[:], W3[:], ACT.Copy).then_inc(w_high, 1)
                        for j in range(2):
                            act.wait_ge(num_ready, j + 1)
                            nc.scalar.activation(PR[j][:], NUM[j][:], ACT.Exp, scale=-1.0).then_inc(exp_done, 1)

                    @block.tensor
                    def _(pe):
                        if k == 0:
                            pe.wait_ge(loaded["table"], 16)
                            pe.wait_ge(loaded["gate"], 16)

                        def turn(b):
                            pe.wait_ge(xn_ready, b * TPB + TPB)
                            some_wait(pe, xt_ready, b - 1)
                            for u in range(TPB):
                                last = nc.tensor.transpose(TP[b % 2][:, u * P:(u + 1) * P], XN[:, b * TPB + u, :], IDENT)
                            last.then_inc(turned, 1)

                        turn(0)
                        for b in range(B):
                            if b + 1 < B:
                                turn(b + 1)
                            pe.wait_ge(xt_ready, b + 1)
                            for u in range(TPB):
                                last = nc.tensor.matmul(LG[:, b * TPB + u, :], XT[:, b % 2, u * P:(u + 1) * P], GW[:],
                                                        start=True, stop=True)
                            last.then_inc(logits_done, 1)
                        pe.wait_ge(choice_ready, 1)
                        q = Q[:].rearrange("p t e -> p (t e)")
                        nc.tensor.matmul(RK[:, 0, :, :].rearrange("p t e -> p (t e)"), BEFORE, q, start=True, stop=True)
                        nc.tensor.matmul(RK[:, 1, :, :].rearrange("p t e -> p (t e)"), ONES, q, start=True,
                                         stop=True).then_inc(ranks_done, 1)
                        pe.wait_ge(tile_t, 1)
                        for t in range(TILES):
                            if t % TPP == 0:
                                pe.wait_ge(rows_ready, t // TPP + 1)
                            for j in range(2):
                                last = nc.tensor.matmul(INV[:].rearrange("p a b -> p (a b)"), ROW1[:, t, j, :],
                                                        TILEX[:, t, j].rearrange("p a b -> p (a b)"),
                                                        start=(t == 0 and j == 0), stop=(t == TILES - 1 and j == 1))
                        last.then_inc(inverse_done, 1)

                    @block.gpsimd
                    def _(pool):
                        if k == 0:
                            for i, (w, high) in enumerate(((W1, W1H), (W3, W3H))):
                                pool.wait_ge(w_high, i + 1)
                                nc.gpsimd.tensor_tensor(w[:].bitcast(F32R), w[:], high[:].bitcast(F32), ALU.subtract)
                        pool.wait_ge(tiles_ready, 1)
                        nc.gpsimd.tensor_tensor(
                            TILEX[:, :, :, 1, :], TILE1[:],
                            TILENO[:].unsqueeze(2).unsqueeze(3).broadcast_to([P, TILES, 2, SLOT_TILES]),
                            ALU.mult).then_inc(tile_t, 1)

        def run_experts(n, EID, TOKEN, AL, NUM, PR, M):
            IN = OUT = UNROLL = 8
            with ExitStack() as c:
                XB = sb(n + "XB", [P, IN, D], F32, c)
                XH, XL = (sb(n + s, [P, 2, P], F32R, c) for s in ("XH", "XL"))
                G = sb(n + "G", [P, 2, FF], F32, c)
                H = sb(n + "H", [P, 2, FF], F32, c)
                HT = sb(n + "HT", [P, 2, FF], F32, c)
                Y = sb(n + "Y", [P, OUT, D], F32, c)
                KEEP = sb(n + "KEEP", [P, TILES, E], F32, c)
                SUM = sb(n + "SUM", [P, TILES], F32, c)
                gp = [ps(f"{n}gp{h}", [P, FF], F32, c) for h in range(2)]
                up = [ps(f"{n}up{h}", [P, FF], F32, c) for h in range(2)]
                hp = [ps(f"{n}hp{h}", [P, FF], F32, c) for h in range(2)]
                xp = ps(n + "xp", [P, FF], F32, c)
                yp = ps(n + "yp", [P, FF], F32, c)
                rows_in = [sem(f"{n}rows_in{u}") for u in range(IN)]
                rows_out = [sem(f"{n}rows_out{u}") for u in range(OUT)]
                (x_turned, high_ready, low_ready, g_done, silu_done, u_done, h_ready, h_turned, ht_ready, y_done, y_ready,
                 weight_link) = (sem(n + s) for s in (
                    "x_turned", "high_ready", "low_ready", "g_done", "silu_done", "u_done", "h_ready", "h_turned",
                    "ht_ready", "y_done", "y_ready", "weight_link"))
                ys_t = YS.rearrange("(i p) d -> p i d", p=P)
                ROUNDS = SLOT_TILES // UNROLL

                def over_tiles(eng, step):
                    def round_of(r, last):
                        for u in range(UNROLL):
                            step(r * UNROLL + u, u, r, last and u == UNROLL - 1)

                    round_of(0, False)
                    round_of(1, False)
                    with eng.Fori(2, ROUNDS - 1) as r:
                        round_of(r, False)
                    round_of(ROUNDS - 1, True)

                with nc.Block() as block:
                    @block.sync
                    def _(sp):
                        def step(i, u, r, last):
                            sp.wait_ge(y_ready, i + 1)
                            sp.dma_start(ys_t[:, bass.ds(i, 1), :], Y[:, u, :]).then_inc(rows_out[u], 16)

                        over_tiles(sp, step)
                        for u in range(OUT):
                            sp.wait_ge(rows_out[u], 16 * ROUNDS)

                    @block.gpsimd
                    def _(pool):
                        for i in range(SLOT_TILES):
                            some_wait(pool, x_turned, i - IN + 1)
                            nc.gpsimd.indirect_dma_start(
                                XB[:, i % IN, :], None, XS,
                                bass.IndirectOffsetOnAxis(ap=TOKEN[:, i:i + 1], axis=0)).then_inc(rows_in[i % IN], 16)

                    @block.vector
                    def _(dve):
                        def low_x(i, u):
                            dve.wait_ge(high_ready, i + 1)
                            some_wait(dve, u_done, i - 1)
                            nc.vector.tensor_tensor(XL[:, u % 2, :], xp[:, 0:P], XH[:, u % 2, :].bitcast(F32),
                                                    ALU.subtract).then_inc(low_ready, 1)

                        def token_weights(i):
                            j, part = i // 4, i % 4
                            ch = Chain(dve, weight_link, j * 6 + (0, 2, 4, 5)[part])
                            if part == 0:
                                ch.link(nc.vector.tensor_tensor(KEEP[:], AL[:],
                                                                M[j][:].unsqueeze(2).broadcast_to([P, TILES, E]), ALU.max))
                                ch.link(nc.vector.scalar_tensor_tensor(out=KEEP[:], in0=KEEP[:], scalar=0.02,
                                                                       in1=NUM[j][:], op0=ALU.mult, op1=ALU.is_ge))
                            if part == 1:
                                ch.link(nc.vector.tensor_tensor(KEEP[:], KEEP[:], PR[j][:], ALU.mult))
                                ch.link(nc.vector.tensor_reduce(SUM[:], KEEP[:], axis=AX.X, op=ALU.add))
                            if part == 2:
                                ch.link(nc.vector.tensor_scalar(SUM[:], SUM[:], 2.0, None, ALU.mult))
                            if part == 3:
                                ch.link(nc.vector.reciprocal(WT[j][:], SUM[:]))

                        def h_copy(j, v):
                            dve.wait_ge(h_turned, j + 1)
                            some_wait(dve, y_done, j - 1)
                            nc.vector.tensor_copy(HT[:, v % 2, :], hp[v % 2][:]).then_inc(ht_ready, 1)

                        low_x(0, 0)

                        def step(i, u, r, last):
                            if not last:
                                low_x(i + 1, u + 1)
                            dve.wait_ge(silu_done, i + 1)
                            dve.wait_ge(u_done, i + 1)
                            some_wait(dve, h_turned, i - 1)
                            nc.vector.tensor_tensor(H[:, u % 2, :], up[u % 2][:], G[:, u % 2, :],
                                                    ALU.mult).then_inc(h_ready, 1)
                            if not isinstance(i, int) or i > 0:
                                h_copy(i - 1, (u - 1) % UNROLL)
                            if isinstance(i, int) and i < 8:
                                token_weights(i)

                        over_tiles(dve, step)
                        h_copy(SLOT_TILES - 1, UNROLL - 1)

                    @block.scalar
                    def _(act):
                        nc.scalar.preload_act_table(ACT.Silu)

                        def high_x(i, u):
                            act.wait_ge(x_turned, i + 1)
                            some_wait(act, u_done, i - 1)
                            nc.scalar.activation(XH[:, u % 2, :], xp[:, 0:P], ACT.Copy).then_inc(high_ready, 1)

                        def y_copy(j, v, r):
                            act.wait_ge(y_done, j + 1)
                            some_wait(act, rows_out[v], 16 * r)
                            nc.scalar.activation(Y[:, v, :], yp[:, 0:D], ACT.Copy).then_inc(y_ready, 1)

                        high_x(0, 0)

                        def step(i, u, r, last):
                            act.wait_ge(g_done, i + 1)
                            some_wait(act, h_ready, i - 1)
                            nc.scalar.activation(G[:, u % 2, :], gp[u % 2][:], ACT.Silu).then_inc(silu_done, 1)
                            if not last:
                                high_x(i + 1, u + 1)
                            if not isinstance(i, int) or i > 1:
                                y_copy(i - 2, (u - 2) % UNROLL, r if u > 1 else r - 1)

                        over_tiles(act, step)
                        y_copy(SLOT_TILES - 2, UNROLL - 2, ROUNDS - 1)
                        y_copy(SLOT_TILES - 1, UNROLL - 1, ROUNDS - 1)

                    @block.tensor
                    def _(pe):
                        def turn_x(i, u, r):
                            pe.wait_ge(rows_in[u], 16 * r + 16)
                            some_wait(pe, low_ready, i)
                            nc.tensor.transpose(xp[:, 0:P], XB[:, u, :], IDENT).then_inc(x_turned, 1)

                        def up_project(bank, i, h, e, high, low, done):
                            expert = bass.ds(e, 1)
                            nc.tensor.matmul(bank[:], XH[:, h, :], high[:, expert, :], start=True, stop=False)
                            nc.tensor.matmul(bank[:], XH[:, h, :], low[:, expert, :].bitcast(F32R), start=False,
                                             stop=False)
                            pe.wait_ge(low_ready, i + 1)
                            nc.tensor.matmul(bank[:], XL[:, h, :], high[:, expert, :], start=False,
                                             stop=True).then_inc(done, 1)

                        def turn_h(j, h):
                            pe.wait_ge(h_ready, j + 1)
                            some_wait(pe, ht_ready, j - 1)
                            for f in range(FC):
                                last = nc.tensor.transpose(hp[h][:, f * P:(f + 1) * P], H[:, h, f * P:(f + 1) * P],
                                                           IDENT)
                            last.then_inc(h_turned, 1)

                        def down_project(j, h, e):
                            pe.wait_ge(ht_ready, j + 1)
                            some_wait(pe, y_ready, j)
                            for f in range(FC):
                                last = nc.tensor.matmul(yp[:, 0:D], HT[:, h, f * P:(f + 1) * P],
                                                        W2[:, bass.ds(e, 1), f, :], start=(f == 0), stop=(f == FC - 1))
                            last.then_inc(y_done, 1)

                        turn_x(0, 0, 0)

                        def expert_of(i):
                            return pe.value_load(EID[0:1, bass.ds(i, 1)], min_val=0, max_val=E - 1)

                        held = {}
                        carried = {place: pe.alloc_register(f"{n}expert{place + 2}") for place in (-2, -1, 0)}

                        def step(i, u, r, last):
                            h = u % 2
                            prev = not isinstance(i, int) or i > 0
                            before = not isinstance(i, int) or i > 1
                            if u == 0:
                                held.clear()
                                held.update({place: pe.snap(carried[place], min_val=0, max_val=E - 1) for place in carried} if before
                                            else {0: expert_of(i)})
                            pe.wait_ge(high_ready, i + 1)
                            some_wait(pe, silu_done, i - 1)
                            up_project(gp[h], i, h, held[u], W1H, W1, g_done)
                            if not last:
                                turn_x(i + 1, (u + 1) % IN, r + (u + 1) // UNROLL)
                            if prev:
                                turn_h(i - 1, 1 - h)
                            some_wait(pe, h_ready, i - 1)
                            up_project(up[h], i, h, held[u], W3H, W3, u_done)
                            if before:
                                down_project(i - 2, h, held[u - 2])
                            if not last:
                                held[u + 1] = expert_of(i + 1)
                            if u + 1 == UNROLL and not last:
                                for place in (-2, -1, 0):
                                    pe.reg_mov(carried[place], held[UNROLL + place])

                        over_tiles(pe, step)
                        turn_h(SLOT_TILES - 1, 1)
                        down_project(SLOT_TILES - 2, 0, held[UNROLL - 2])
                        down_project(SLOT_TILES - 1, 1, held[UNROLL - 1])

        def combine(n, c):
            BUF = 2 * 2 * TPB
            GB = sb(n + "GB", [P, BUF, D], F32, c)
            ACC = sb(n + "ACC", [P, TPB, D], F32, c)
            fetched = [sem(f"{n}fetched{u}") for u in range(BUF)]
            half_sum, added = sem(n + "half_sum"), sem(n + "added")

            def on_pool(pool, b, tiles=range(TPB)):
                for u in tiles:
                    some_wait(pool, added, (b - 2) * TPB + u + 1)
                    for j in range(2):
                        t, at = b * TPB + u, (b % 2 * TPB + u) * 2 + j
                        nc.gpsimd.indirect_dma_start(
                            GB[:, at, :], None, YS,
                            bass.IndirectOffsetOnAxis(ap=SLOT[j][:, t:t + 1], axis=0)).then_inc(fetched[at], 16)

            def on_vector(dve, b, h):
                rounds = (b - h) // 2
                some_wait(dve, added, b * TPB)
                for u in range(TPB):
                    t, at = b * TPB + u, (h * TPB + u) * 2
                    dve.wait_ge(fetched[at], rounds * 16 + 16)
                    nc.vector.scalar_tensor_tensor(
                        out=ACC[:, u, :], in0=GB[:, at, :], scalar=WT[0][:, bass.ds(t, 1)],
                        in1=X[:, bass.ds(t, 1), :], op0=ALU.mult, op1=ALU.add).then_inc(half_sum, 1)
                for u in range(TPB):
                    t, at = b * TPB + u, (h * TPB + u) * 2 + 1
                    dve.wait_ge(fetched[at], rounds * 16 + 16)
                    dve.wait_ge(half_sum, b * TPB + u + 1)
                    nc.vector.scalar_tensor_tensor(
                        out=X[:, bass.ds(t, 1), :], in0=GB[:, at, :], scalar=WT[1][:, bass.ds(t, 1)],
                        in1=ACC[:, u, :], op0=ALU.mult, op1=ALU.add).then_inc(added, 1)

            def x_ready(dve, b):
                dve.wait_ge(added, b * TPB + TPB)

            return on_pool, on_vector, x_ready

        def scan_layer(combine_n):
            n = "s_"
            with ExitStack() as c:
                ln = layernorm(n + "ln", c, roots=2, tables=True)
                gather, combine_vector, x_summed = combine(combine_n, c) if combine_n else (None, None, None)
                tile = lambda name, shape: sb(n + name, shape, F32, c)
                R1P = tile("R1P", [P, 2, TPB])
                CONVD, INP = tile("CONVD", [P, KC, P]), tile("INP", [P, 4, P])
                MIX, OUTP = tile("MIX", [P, P]), tile("OUTP", [P, P])
                XN = tile("XN", [P, 2, TPB, D])
                CV = tile("CV", [P, 2, KC - 1 + S])
                XC = tile("XC", [P, 2, S])
                wide = lambda name: tile(name, [P, S])
                SC, EDT, EDT1, LDT, DT, GATE, ROT1, ROT2, ROT, VIN, LD, LS, E1, E2, TV, CS, CK, FIN, FG = (
                    wide(s) for s in ("SC", "EDT", "EDT1", "LDT", "DT", "GATE", "ROT1", "ROT2",
                                      "ROT", "VIN", "LD", "LS", "E1", "E2", "TV", "CS", "CK", "FIN", "FG"))
                small = lambda name: tile(name, [P, CHUNKS])
                BOUT, LAST, CD, NCD, EN, EP, FIRST, SEED, SUM, CARRY = (small(s) for s in (
                    "BOUT", "LAST", "CD", "NCD", "EN", "EP", "FIRST", "SEED", "SUM", "CARRY"))
                tp, cv, pdt, pv, pvs, pg, mp, op = (ps(n + s, [P, S], F32, c) for s in (
                    "tp", "cv", "pdt", "pv", "pvs", "pg", "mp", "op"))
                (weights_in, pads_set, xn_ready, turned, scaled, clipped, conv_done, conv_sig,
                 xc_ready, proj_done, x_plus, dt_exp, dt_low, dt_ln, dt_ready, gate_ready,
                 turned_v, vin_ready, ls_ready, e_ready, cs_ready, small_ready, small_exp, fin_ready, mixed, fg_ready,
                 projected, x_done, chain_b, chain_p, chain_0) = (sem(n + s) for s in (
                    "weights_in", "pads_set", "xn_ready", "turned", "scaled", "clipped", "conv_done",
                    "conv_sig", "xc_ready", "proj_done", "x_plus", "dt_exp", "dt_low", "dt_ln", "dt_ready", "gate_ready", "turned_v", "vin_ready", "ls_ready", "e_ready", "cs_ready", "small_ready",
                    "small_exp", "fin_ready", "mixed", "fg_ready", "projected", "x_done", "chain_b",
                    "chain_p", "chain_0"))
                by_chunk = lambda v: v.rearrange("p (c n) -> p c n", n=CHUNK)
                spread = lambda v: v.unsqueeze(2).broadcast_to([P, CHUNKS, CHUNK])
                NEWCHUNK = CT[:, CONST["newchunk"]]

                with nc.Block() as block:
                    @block.sync
                    def _(sp):
                        sp.dma_start(CONVD[:], conv_diag).then_inc(weights_in, 16)
                        sp.dma_start(INP[:], in_proj).then_inc(weights_in, 16)
                        sp.dma_start(MIX[:], head_mix).then_inc(weights_in, 16)
                        sp.dma_start(OUTP[:], out_proj).then_inc(weights_in, 16)
                        sp.wait_ge(weights_in, 64)

                    @block.vector
                    def _(dve):
                        nc.vector.memset(CV[:, :, 0:KC - 1], 0.0).then_inc(pads_set, 1)
                        nc.vector.memset(CARRY[:, 0:1], 0.0).then_inc(pads_set, 1)

                        NB = 13

                        def body(b, h, a, c):
                            ah = 1 - h
                            if a is not None:
                                dve.wait_ge(scaled, a + 1)
                                nc.vector.tensor_scalar(CV[:, ah, KC - 1:], CV[:, ah, KC - 1:], 60000.0, -60000.0,
                                                        ALU.min, ALU.max).then_inc(clipped, 1)
                            if b is not None:
                                cb = Chain(dve, chain_b, b * NB)
                                dve.wait_ge(dt_ln, b + 1)
                                nc.vector.tensor_scalar(DT[:], LDT[:], 0.001, 2.0, ALU.max, ALU.min).then_inc(dt_ready, 1)
                                dve.wait_ge(dt_ready, b + 1)
                                cb.link(nc.vector.tensor_tensor_scan(out=LD[:], data0=NEWCHUNK, data1=DT[:],
                                                                     initial=0.0, op0=ALU.mult, op1=ALU.add))
                                cb.link(nc.vector.tensor_scalar(LD[:], LD[:], 20.0, None, ALU.min))
                                nc.vector.tensor_tensor(by_chunk(LS[:]), by_chunk(LD[:]),
                                                        by_chunk(LD[:])[:, :, 0:1].broadcast_to([P, CHUNKS, CHUNK]),
                                                        ALU.subtract).then_inc(ls_ready, 1)
                                cb.link(nc.vector.tensor_copy(LAST[:], by_chunk(LD[:])[:, :, CHUNK - 1]))
                                cb.link(nc.vector.tensor_tensor_scan(
                                    out=CD[:], data0=CT[:, CONST["ones"]][:, 0:CHUNKS], data1=LAST[:], initial=0.0,
                                    op0=ALU.mult, op1=ALU.add))
                                cb.link(nc.vector.tensor_scalar(CD[:], CD[:], 80.0, None, ALU.min))
                                nc.vector.tensor_scalar(NCD[:], CD[:], CD[:, 0:1], 20.0, ALU.subtract,
                                                        ALU.min).then_inc(small_ready, 1)
                            if c is not None and combine_vector is not None:
                                combine_vector(dve, c, h)
                                x_summed(dve, c)
                            if a is not None:
                                dve.wait_ge(conv_sig, a + 1)
                                some_wait(dve, proj_done, a - 1)
                                nc.vector.scalar_tensor_tensor(out=XC[:, ah, :], in0=cv[:], scalar=CONV_B, in1=SC[:],
                                                               op0=ALU.add, op1=ALU.mult).then_inc(xc_ready, 1)
                            if c is not None:
                                ln.stats(dve, c, h, lambda u: X[:, bass.ds(c * TPB + u, 1), :])
                            if b is not None:
                                dve.wait_ge(e_ready, b + 1)
                                dve.wait_ge(vin_ready, b + 1)
                                cb.link(nc.vector.tensor_tensor(TV[:], E1[:], VIN[:], ALU.mult))
                                cb.link(nc.vector.tensor_tensor_scan(out=CS[:], data0=NEWCHUNK, data1=TV[:],
                                                                     initial=0.0, op0=ALU.mult, op1=ALU.add))
                                cb.link(nc.vector.tensor_tensor(BOUT[:], by_chunk(CS[:])[:, :, CHUNK - 1],
                                                                by_chunk(E2[:])[:, :, CHUNK - 1], ALU.mult))
                                dve.wait_ge(small_exp, b + 1)
                                cb.link(nc.vector.tensor_tensor(SEED[:], BOUT[:], EN[:], ALU.mult))
                                cb.link(nc.vector.tensor_tensor_scan(
                                    out=SUM[:], data0=CT[:, CONST["ones"]][:, 0:CHUNKS], data1=SEED[:], initial=0.0,
                                    op0=ALU.mult, op1=ALU.add))
                                cb.link(nc.vector.tensor_tensor(CARRY[:, 1:], SUM[:, 0:CHUNKS - 1], EP[:, 1:], ALU.mult))
                                cb.link(nc.vector.tensor_tensor(CARRY[:, 1:], CARRY[:, 1:], FIRST[:, 1:], ALU.mult))
                                cb.link(nc.vector.tensor_tensor(by_chunk(CK[:]), by_chunk(CS[:]), spread(CARRY[:]),
                                                                ALU.add))
                                nc.vector.tensor_tensor(FIN[:], E2[:], CK[:], ALU.mult).then_inc(fin_ready, 1)
                            if a is not None:
                                dve.wait_ge(dt_exp, a + 1)
                                nc.vector.tensor_scalar(EDT1[:], EDT[:], 1e4, 1.0, ALU.min, ALU.add).then_inc(dt_low, 1)
                                some_wait(dve, chain_p, a)
                                nc.vector.tensor_tensor(ROT1[:], pv[:], CT[:, CONST["cos"]],
                                                        ALU.mult).then_inc(turned_v, 1)
                                nc.vector.tensor_tensor(ROT2[:], pvs[:], CT[:, CONST["sin"]],
                                                        ALU.mult).then_inc(turned_v, 1)
                            if b is not None:
                                dve.wait_ge(mixed, b + 1)
                                dve.wait_ge(gate_ready, b + 1)
                                some_wait(dve, projected, b)
                                nc.vector.tensor_tensor(FG[:], mp[:], GATE[:], ALU.mult).then_inc(fg_ready, 1)
                            if c is not None:
                                dve.wait_ge(ln.ready, c + 1)
                                nc.vector.tensor_scalar(R1P[:, h, :], ln.roots[:, h, 0, :], 1.0, None, ALU.add)
                                some_wait(dve, turned, c - 1)
                                for u in range(TPB):
                                    nc.vector.tensor_scalar(XN[:, h, u, :], X[:, bass.ds(c * TPB + u, 1), :],
                                                            ln.mean(h, u), ln.rstd(h, u, 1), ALU.subtract,
                                                            ALU.mult).then_inc(xn_ready, 1)
                            if b is not None:
                                dve.wait_ge(projected, b + 1)
                                dve.wait_ge(x_plus, b * TPB + TPB)
                                xb = X[:, bass.ds(b * TPB, TPB), :].rearrange("p t d -> p (t d)")
                                nc.vector.tensor_tensor(xb, op[:], xb, ALU.add).then_inc(x_done, 1)
                                assert cb.n == NB, cb.n

                        over_batches(dve, body)
                        dve.wait_ge(x_done, B)

                    @block.scalar
                    def _(act):
                        nc.scalar.preload_act_table_set(LN_EXP)
                        act.wait_ge(pads_set, 2)

                        def body(b, h, a, c):
                            if b is not None:
                                act.wait_ge(proj_done, b + 1)
                                some_wait(act, fg_ready, b)
                                nc.scalar.activation(GATE[:], pg[:], ACT.Sigmoid).then_inc(gate_ready, 1)
                            if a is not None:
                                act.wait_ge(conv_done, a + 1)
                                some_wait(act, xc_ready, a)
                                nc.scalar.activation(SC[:], cv[:], ACT.Sigmoid, bias=CONV_B).then_inc(conv_sig, 1)
                            nc.scalar.preload_act_table_set(LN_EXP)
                            if b is not None:
                                act.wait_ge(ls_ready, b + 1)
                                some_wait(act, fin_ready, b)
                                nc.scalar.activation(E1[:], LS[:], ACT.Exp)
                                nc.scalar.activation(E2[:], LS[:], ACT.Exp, scale=-1.0).then_inc(e_ready, 1)
                                act.wait_ge(small_ready, b + 1)
                                nc.scalar.activation(FIRST[:], by_chunk(LD[:])[:, :, 0], ACT.Exp, scale=-1.0)
                                nc.scalar.activation(EN[:], NCD[:], ACT.Exp)
                                nc.scalar.activation(EP[:], NCD[:], ACT.Exp, scale=-1.0).then_inc(small_exp, 1)
                            if a is not None:
                                act.wait_ge(proj_done, a + 1)
                                some_wait(act, dt_low, a)
                                nc.scalar.activation(EDT[:], pdt[:], ACT.Exp, bias=DT_BIAS).then_inc(dt_exp, 1)
                                act.wait_ge(dt_low, a + 1)
                                some_wait(act, dt_ready, a)
                                nc.scalar.activation(LDT[:], EDT1[:], ACT.Ln).then_inc(dt_ln, 1)
                            if c is not None:
                                ln.guess(act, c, h)
                            if a is not None:
                                act.wait_ge(xn_ready, a * TPB + TPB)
                                for u in range(TPB):
                                    t = a * TPB + u
                                    nc.scalar.activation(X[:, bass.ds(t, 1), :], X[:, bass.ds(t, 1), :], ACT.Identity,
                                                         scale=R1P[:, 1 - h, u:u + 1],
                                                         bias=ln.minus(1 - h, u)).then_inc(x_plus, 1)
                            if c is not None:
                                act.wait_ge(turned, c + 1)
                                some_wait(act, conv_done, c - 1)
                                nc.scalar.activation(CV[:, h, KC - 1:], tp[:], ACT.Identity,
                                                     scale=NORM_SCALE).then_inc(scaled, 1)

                        over_batches(act, body)

                    @block.gpsimd
                    def _(pool):
                        if gather is not None:
                            gather(pool, 0)

                        def body(b, h, a, c):
                            more = gather is not None and c is not None and c + 1 < B
                            if b is not None:
                                pool.wait_ge(chain_p, b + 1)
                                pool.wait_ge(dt_ready, b + 1)
                                nc.gpsimd.tensor_tensor(VIN[:], ROT[:], DT[:], ALU.mult).then_inc(vin_ready, 1)
                            if more and c > 0:
                                gather(pool, c + 1, range(TPB - 1))
                            if c is not None:
                                some_wait(pool, x_plus, (c - 1) * TPB)
                                ln.finish(pool, nc.gpsimd, c, h)
                            if a is not None:
                                pool.wait_ge(turned_v, 2 * a + 2)
                                some_wait(pool, vin_ready, a)
                                nc.gpsimd.tensor_tensor(ROT[:], ROT1[:], ROT2[:], ALU.add).then_inc(chain_p, 1)
                            if more:
                                gather(pool, c + 1, range(TPB - 1 if c > 0 else 0, TPB))

                        over_batches(pool, body, unroll=True)

                    @block.tensor
                    def _(pe):
                        pe.wait_ge(weights_in, 64)

                        def body(b, h, a, c):
                            ah = 1 - h
                            if a is not None:
                                pe.wait_ge(clipped, a + 1)
                                some_wait(pe, xc_ready, a)
                                for w in range(KC):
                                    last = nc.tensor.matmul(cv[:], CONVD[:, w, :], CV[:, ah, w:w + S], start=(w == 0),
                                                            stop=(w == KC - 1))
                                last.then_inc(conv_done, 1)
                            if a is not None:
                                pe.wait_ge(xc_ready, a + 1)
                                some_wait(pe, dt_exp, a)
                                some_wait(pe, gate_ready, a)
                                some_wait(pe, turned_v, 2 * a)
                                for w, bank in enumerate((pdt, pg, pv, pvs)):
                                    last = nc.tensor.matmul(bank[:], INP[:, w, :], XC[:, ah, :], start=True, stop=True)
                                last.then_inc(proj_done, 1)
                            if b is not None:
                                pe.wait_ge(fin_ready, b + 1)
                                some_wait(pe, fg_ready, b)
                                nc.tensor.matmul(mp[:], MIX[:], FIN[:], start=True, stop=True).then_inc(mixed, 1)
                                pe.wait_ge(fg_ready, b + 1)
                                some_wait(pe, x_done, b)
                                for u in range(TPB):
                                    last = nc.tensor.matmul(op[:, u * P:(u + 1) * P], FG[:, u * P:(u + 1) * P],
                                                            OUTP[:], start=True, stop=True)
                                last.then_inc(projected, 1)
                            if c is not None:
                                pe.wait_ge(xn_ready, c * TPB + TPB)
                                some_wait(pe, scaled, c)
                                for u in range(TPB):
                                    last = nc.tensor.transpose(tp[:, u * P:(u + 1) * P], XN[:, h, u, :], IDENT)
                                last.then_inc(turned, 1)

                        over_batches(pe, body)

        def shifted_ffn(k, combine_n=None):
            n = f"f{k}_"
            with ExitStack() as c:
                ln = layernorm(n + "ln", c)
                gather, combine_vector, x_summed = combine(combine_n, c) if combine_n else (None, None, None)
                tile = lambda name, shape: sb(n + name, shape, F32, c)
                FW = tile("FW", [P, 3, P])
                WR, WK = tile("WR", [P, 2, P]), tile("WK", [P, 2, P])
                XN = tile("XN", [P, 2, TPB, D])
                Z = tile("Z", [P, 2, 1 + S])
                KR, KA, TMP = (tile(s, [P, S]) for s in ("KR", "KA", "TMP"))
                R = tile("R", [P, 2, S])
                tp, kp, rp, vp = (ps(n + s, [P, S], F32, c) for s in ("tp", "kp", "rp", "vp"))
                (weights_in, w_ready, pads_set, xn_ready, turned, z_ready, k_done, r_done, k_relu, ka_ready, r_ready,
                 v_done, x_done, chain_b, chain_0) = (sem(n + s) for s in (
                    "weights_in", "w_ready", "pads_set", "xn_ready", "turned", "z_ready", "k_done", "r_done", "k_relu",
                    "ka_ready", "r_ready", "v_done", "x_done", "chain_b", "chain_0"))

                with nc.Block() as block:
                    @block.sync
                    def _(sp):
                        sp.dma_start(FW[:], ffn_w).then_inc(weights_in, 16)
                        sp.wait_ge(weights_in, 16)

                    @block.vector
                    def _(dve):
                        nc.vector.memset(Z[:, :, 0:1], 0.0).then_inc(pads_set, 1)
                        dve.wait_ge(weights_in, 16)
                        ch = Chain(dve, chain_0)
                        ch.link(nc.vector.tensor_scalar(VEC[:, 5:7], VEC[:, 3:5], -1.0, 1.0, ALU.mult, ALU.add))
                        for w, (dst, mu) in enumerate(((WR, MU_R), (WK, MU_K))):
                            nc.vector.tensor_scalar(dst[:, 0, :], FW[:, w, :], mu, None, ALU.mult).then_inc(w_ready, 1)
                            nc.vector.tensor_scalar(dst[:, 1, :], FW[:, w, :], VEC[:, 5 + w:6 + w], None,
                                                    ALU.mult).then_inc(w_ready, 1)

                        def body(b, h, a, c):
                            if c is not None and combine_vector is not None:
                                combine_vector(dve, c, h)
                                x_summed(dve, c)
                            if b is not None:
                                dve.wait_ge(k_relu, b + 1)
                                some_wait(dve, v_done, b)
                                nc.vector.tensor_tensor(KA[:], kp[:], KR[:], ALU.mult).then_inc(ka_ready, 1)
                            if c is not None:
                                ln.stats(dve, c, h, lambda u: X[:, bass.ds(c * TPB + u, 1), :])
                                some_wait(dve, xn_ready, (c - 1) * TPB)
                                ln.finish(dve, nc.vector, c, h)
                            if b is not None:
                                cb = Chain(dve, chain_b, b * 1)
                                dve.wait_ge(r_ready, b + 1)
                                dve.wait_ge(v_done, b + 1)
                                cb.link(nc.vector.scalar_tensor_tensor(out=TMP[:], in0=vp[:], scalar=0.5, in1=R[:, h, :],
                                                                       op0=ALU.mult, op1=ALU.mult))
                                xb = X[:, bass.ds(b * TPB, TPB), :].rearrange("p t d -> p (t d)")
                                nc.vector.tensor_tensor(xb, xb, TMP[:], ALU.add).then_inc(x_done, 1)

                        over_batches(dve, body)
                        dve.wait_ge(x_done, B)

                    @block.scalar
                    def _(act):
                        nc.scalar.preload_act_table(ACT.Sigmoid)
                        act.wait_ge(pads_set, 1)

                        def body(b, h, a, c):
                            if b is not None:
                                act.wait_ge(k_done, b + 1)
                                some_wait(act, ka_ready, b)
                                nc.scalar.activation(KR[:], kp[:], ACT.Relu).then_inc(k_relu, 1)
                                act.wait_ge(r_done, b + 1)
                                some_wait(act, x_done, b - 1)
                                nc.scalar.activation(R[:, h, :], rp[:], ACT.Sigmoid).then_inc(r_ready, 1)
                            if a is not None:
                                act.wait_ge(turned, a + 1)
                                some_wait(act, r_done, a - 1)
                                nc.scalar.activation(Z[:, 1 - h, 1:], tp[:], ACT.Copy).then_inc(z_ready, 1)
                            if c is not None:
                                act.wait_ge(ln.ready, c + 1)
                                some_wait(act, turned, c - 1)
                                for u in range(TPB):
                                    nc.scalar.activation(XN[:, h, u, :], X[:, bass.ds(c * TPB + u, 1), :], ACT.Identity,
                                                         scale=ln.rstd(h, u), bias=ln.minus(h, u)).then_inc(xn_ready, 1)

                        over_batches(act, body)

                    @block.gpsimd
                    def _(pool):
                        if gather is not None:
                            for b in range(B):
                                gather(pool, b)

                    @block.tensor
                    def _(pe):
                        pe.wait_ge(w_ready, 4)

                        def body(b, h, a, c):
                            if b is not None:
                                pe.wait_ge(z_ready, b + 1)
                                some_wait(pe, ka_ready, b)
                                nc.tensor.matmul(kp[:], WK[:, 0, :], Z[:, h, 1:], start=True, stop=False)
                                nc.tensor.matmul(kp[:], WK[:, 1, :], Z[:, h, 0:S], start=False,
                                                 stop=True).then_inc(k_done, 1)
                                some_wait(pe, r_ready, b)
                                for u in range(TPB):
                                    nc.tensor.matmul(rp[:, u * P:(u + 1) * P], Z[:, h, 1 + u * P:1 + (u + 1) * P],
                                                     WR[:, 0, :], start=True, stop=False)
                                    last = nc.tensor.matmul(rp[:, u * P:(u + 1) * P], Z[:, h, u * P:(u + 1) * P],
                                                            WR[:, 1, :], start=False, stop=True)
                                last.then_inc(r_done, 1)
                            if a is not None:
                                pe.wait_ge(xn_ready, a * TPB + TPB)
                                some_wait(pe, z_ready, a)
                                for u in range(TPB):
                                    last = nc.tensor.transpose(tp[:, u * P:(u + 1) * P], XN[:, 1 - h, u, :], IDENT)
                                last.then_inc(turned, 1)
                            if b is not None:
                                pe.wait_ge(ka_ready, b + 1)
                                some_wait(pe, x_done, b)
                                for u in range(TPB):
                                    last = nc.tensor.matmul(vp[:, u * P:(u + 1) * P], KA[:, u * P:(u + 1) * P],
                                                            FW[:, 2, :], start=True, stop=True)
                                last.then_inc(v_done, 1)

                        over_batches(pe, body)

        def attention():
            n = "a_"
            STEPS = B * GROUPS
            QUNITS = [(3, j, 1, 4 * P) for j in range(4)] + [(2, j, 1, 3 * P) for j in range(4)] + \
                     [(1, 0, 2, 2 * P), (1, 2, 2, 2 * P), (0, 0, 4, P)]
            KUNITS = [(TPB - 1 - qt, j, m, w) for qt, j, m, w in QUNITS]
            KOFF = [0, 4 * P, 7 * P, 9 * P]
            SCALE = 1.0 / math.sqrt(DK)
            NU = len(QUNITS)
            SR, TR = 3, 2
            with ExitStack() as c:
                ln = layernorm(n + "ln", c)
                tile = lambda name, shape, dt=F32: sb(n + name, shape, dt, c)
                WH, WL = (tile(s, [P, 2 * GROUPS + 1, P], F32R) for s in ("WH", "WL"))
                WO = tile("WO", [P, P])
                MASKF, MASK = tile("MASKF", [P, 3, P]), tile("MASK", [P, 3, P], BF16)
                XN = tile("XN", [P, TPB, D])
                ZH, ZL = (tile(s, [P, S], F32R) for s in ("ZH", "ZL"))
                PART = tile("PART", [P, S], F32R)
                Q = tile("Q", [P, 2, GROUPS, S], F32R)
                K = tile("K", [P, GROUPS, S], F32R)
                KPAD = tile("KPAD", [P, 2, HA, S], F32R)
                V = tile("V", [P, 2, TPB, HA, QR])
                QM = tile("QM", [P, 2, S], F32R)
                NMAX = tile("NMAX", [P, 2, TPB, GH])
                NHIGH = tile("NHIGH", [P, TPB, GH], F32R)
                SPREAD = tile("SPREAD", [P, TPB, P])
                PT = tile("PT", [P, 2, GH, 10 * P])
                W = PT[:, 0, 0, 0:(2 * GROUPS + 1) * P].rearrange("p (w d) -> p w d", d=P)
                CTX = tile("CTX", [P, S])
                RSUM = tile("RSUM", [P, TPB, GH])
                CN = tile("CN", [P, TPB, P])
                CNT = tile("CNT", [P, S])
                score = [ps(f"{n}score{i}", [P, S], F32, c) for i in range(SR)]
                scoret = [ps(f"{n}scoret{i}", [P, S], F32, c) for i in range(TR)]
                ctxp, mixp, turnp = (ps(n + s, [P, S], F32, c) for s in ("ctxp", "mixp", "turnp"))
                names = ("weights_in", "zeros_set", "mask_ready", "xn_ready", "turned", "z_high", "z_ready", "w_high", "w_ready", "v_done", "v_ready",
                         "qk_done", "part_ready", "qk_ready", "score_done", "max_done", "spread_ready",
                         "spread_turned", "qm_ready", "scoret_done", "exp_done", "ctx_done", "ctx_ready",
                         "ctx_turned", "cn_ready", "cn_turned", "cnt_ready", "out_done", "x_done", "chain_m",
                         "chain_c", "keys_zeroed")
                (weights_in, zeros_set, mask_ready, xn_ready, turned, z_high, z_ready, w_high, w_ready, v_done, v_ready, qk_done, part_ready,
                 qk_ready, score_done, max_done, spread_ready, spread_turned, qm_ready, scoret_done, exp_done,
                 ctx_done, ctx_ready, ctx_turned, cn_ready, cn_turned, cnt_ready, out_done, x_done, chain_m, chain_c,
                 keys_zeroed) = (sem(n + s) for s in names)

                kpad_in = [sem(f"{n}kpad_in{g}") for g in range(GROUPS)]


                def over_steps(eng, step, before):
                    before()
                    for s in range(2 * GROUPS):
                        step(s, s % GROUPS, s // GROUPS % 2, s // GROUPS)
                    with eng.Fori(1, B // 2 - 1) as i:
                        for r in range(2 * GROUPS):
                            step(i * 2 * GROUPS + r, r % GROUPS, r // GROUPS, i * 2 + r // GROUPS)
                    for s in range(STEPS - 2 * GROUPS, STEPS):
                        step(s, s % GROUPS, s // GROUPS % 2, s // GROUPS)

                PROJECT_AT = {(0, 3): (0, 0), (0, 7): (0, 1), (1, 1): (1, 0), (1, 5): (1, 1),
                              (2, 1): (2, 0), (2, 5): (2, 1), (3, 1): (3, 0), (3, 5): (3, 1)}
                first_banks = [mixp] + score + scoret

                def known(s):
                    return isinstance(s, int)

                RING = [[(g * NU + k) % SR for k in range(NU)] for g in range(GROUPS)]
                BATCH_UNITS = GROUPS * NU

                def since(ring, g, k):
                    flat = [x for group in ring for x in group] * 2
                    at = BATCH_UNITS + g * NU + k
                    return next(d for d in range(1, BATCH_UNITS) if flat[at - d] == flat[at])

                RINGT = [[(g * NU + k) % TR for k in range(NU)] for g in range(GROUPS)]

                with nc.Block() as block:
                    @block.sync
                    def _(sp):
                        for dst, src in ((W[:, 0:GROUPS, :], w_q), (W[:, GROUPS:2 * GROUPS, :], w_k),
                                         (W[:, 2 * GROUPS, :], w_v), (WO[:], w_o), (MASKF[:], masks)):
                            sp.dma_start(dst, src).then_inc(weights_in, 16)
                        sp.wait_ge(weights_in, 80)
                        sp.wait_ge(keys_zeroed, 1)

                        for b in range(B):
                            for g in range(GROUPS):
                                sp.wait_ge(qk_ready, 2 * GROUPS * b + 2 * (g + 1))
                                if b >= 2:
                                    sp.wait_ge(scoret_done, (b - 1) * GROUPS * NU)
                                for j in range(GH):
                                    rows = slice(j * QR, (j + 1) * QR)
                                    sp.dma_start(KPAD[rows, b % 2, g * GH + j, :].bitcast(F32),
                                                 K[rows, g, :].bitcast(F32)).then_inc(kpad_in[g], 16)
                        for g in range(GROUPS):
                            sp.wait_ge(kpad_in[g], 16 * GH * B)

                    @block.vector
                    def _(dve):
                        def stats(b, h):
                            ln.stats(dve, b, h, lambda u: X[:, bass.ds(b * TPB + u, 1), :])

                        stats(0, 0)
                        stats(1, 1)
                        nc.vector.memset(V[:], 0.0).then_inc(zeros_set, 1)
                        nc.vector.memset(SPREAD[:], 0.0).then_inc(zeros_set, 1)
                        dve.wait_ge(zeros_set, 2)
                        nc.vector.memset(V[:, :, :, :, DK:DK + 1], 1.0).then_inc(zeros_set, 1)
                        dve.wait_ge(weights_in, 80)
                        nc.vector.tensor_copy(MASK[:], MASKF[:]).then_inc(mask_ready, 1)

                        def normalise(b, h):
                            dve.wait_ge(ln.ready, b + 1)
                            some_wait(dve, turned, b)
                            for u in range(TPB):
                                nc.vector.tensor_scalar(XN[:, u, :], X[:, bass.ds(b * TPB + u, 1), :], ln.mean(h, u),
                                                        ln.rstd(h, u), ALU.subtract, ALU.mult).then_inc(xn_ready, 1)

                        def z_low(b):
                            dve.wait_ge(z_high, b + 1)
                            nc.vector.tensor_tensor(ZL[:], turnp[:], ZH[:].bitcast(F32),
                                                    ALU.subtract).then_inc(z_ready, 1)

                        def split(b, h, g, w, bank=mixp):
                            dve.wait_ge(part_ready, (b * GROUPS + g) * 2 + w + 1)
                            if w == 1:
                                some_wait(dve, kpad_in[g], b * GH * 16)
                            nc.vector.tensor_tensor((Q[:, h, g, :], K[:, g, :])[w], bank[:], PART[:].bitcast(F32),
                                                    ALU.subtract).then_inc(qk_ready, 1)

                        def unit_max(s, g, k):
                            qt, j, m, w = QUNITS[k]
                            dve.wait_ge(score_done, s * NU + k + 1)
                            nc.vector.tensor_reduce(NMAX[:, g % 2, qt, j:j + m],
                                                    score[RING[g][k]][:, 0:m * w].rearrange("p (m w) -> p m w", m=m),
                                                    axis=AX.X, op=ALU.max, negate=True).then_inc(max_done, 1)

                        def spread_max(s, g):
                            cm = Chain(dve, chain_m, s * 2)
                            dve.wait_ge(max_done, (s + 1) * NU)
                            some_wait(dve, spread_turned, s)
                            cm.link(nc.vector.tensor_copy(NHIGH[:], NMAX[:, g % 2, :, :]))
                            columns = SPREAD[:].rearrange("p t (j r) -> p t j r", r=QR)
                            cm.link(nc.vector.tensor_copy(columns[:, :, :, MH_ROW], NHIGH[:].bitcast(F32)))
                            nc.vector.tensor_tensor(columns[:, :, :, ML_ROW], NMAX[:, g % 2, :, :],
                                                    NHIGH[:].bitcast(F32), ALU.subtract).then_inc(spread_ready, 1)

                        def add_max(s, g, h):
                            dve.wait_ge(spread_turned, s + 1)
                            some_wait(dve, scoret_done, (s - 1) * NU)
                            nc.vector.tensor_tensor(QM[:, g % 2, :], turnp[:], Q[:, h, g, :].bitcast(F32),
                                                    ALU.add).then_inc(qm_ready, 1)

                        def normalise_ctx(s, g, b):
                            cc = Chain(dve, chain_c, s)
                            dve.wait_ge(ctx_turned, s + 1)
                            ctx_v = turnp[:].rearrange("p (t j r) -> p t j r", t=TPB, r=QR)
                            cc.link(nc.vector.reciprocal(RSUM[:], ctx_v[:, :, :, DK]))
                            if g == 0:
                                some_wait(dve, cn_turned, b)
                            nc.vector.tensor_tensor(
                                CN[:].rearrange("p t (j d) -> p t j d", d=DK)[:, :, g * GH:(g + 1) * GH, :],
                                ctx_v[:, :, :, 0:DK], RSUM[:].unsqueeze(3).broadcast_to([P, TPB, GH, DK]),
                                ALU.mult).then_inc(cn_ready, 1)

                        def add_out(b):
                            dve.wait_ge(out_done, b + 1)
                            xb = X[:, bass.ds(b * TPB, TPB), :].rearrange("p t d -> p (t d)")
                            nc.vector.tensor_tensor(xb, mixp[:], xb, ALU.add).then_inc(x_done, 1)

                        def before():
                            normalise(0, 0)
                            dve.wait_ge(w_high, 1)
                            nc.vector.tensor_tensor(WL[:], W, WH[:].bitcast(F32), ALU.subtract).then_inc(w_ready, 1)
                            z_low(0)
                            for g in range(GROUPS):
                                for w in range(2):
                                    split(0, 0, g, w, first_banks[(2 * g + w) % len(first_banks)])
                            normalise(1, 1)
                            z_low(1)
                            for s in range(2):
                                for k in range(NU):
                                    unit_max(s, s, k)
                                spread_max(s, s)
                                if s == 0:
                                    add_max(0, 0, 0)

                        def step(s, g, h, b):
                            more = not known(s) or s + 2 < STEPS
                            next_batch = not known(s) or b + 1 < B
                            for k in range(NU):
                                if k == 4 and (not known(s) or s > 0):
                                    normalise_ctx(s - 1, (g - 1) % GROUPS, b if g > 0 else b - 1)
                                if k == 7 and (not known(s) or s + 1 < STEPS):
                                    add_max(s + 1, (g + 1) % GROUPS, h if g < 3 else 1 - h)
                                if k == 0 and g == 3 and (not known(b) or b + 2 < B):
                                    stats(b + 2, h)
                                if k == 8 and g == 3 and (not known(b) or b + 2 < B):
                                    normalise(b + 2, h)
                                if k == 10 and g == 1 and (not known(b) or b > 0):
                                    add_out(b - 1)
                                if next_batch and (g, k - 1) in PROJECT_AT:
                                    split(b + 1, 1 - h, *PROJECT_AT[g, k - 1])
                                if more:
                                    unit_max(s + 2, (g + 2) % GROUPS, k)
                            if g == 3 and (not known(b) or b + 2 < B):
                                z_low(b + 2)
                            if more:
                                spread_max(s + 2, (g + 2) % GROUPS)

                        over_steps(dve, step, before)
                        normalise_ctx(STEPS - 1, GROUPS - 1, B - 1)
                        add_out(B - 1)
                        dve.wait_ge(x_done, B)

                    @block.scalar
                    def _(act):
                        nc.scalar.preload_act_table_set(LN_EXP)
                        act.wait_ge(weights_in, 80)
                        nc.scalar.activation(WH[:], W, ACT.Copy).then_inc(w_high, 1)
                        act.wait_ge(zeros_set, 3)

                        def z_copy(b):
                            act.wait_ge(turned, b + 1)
                            some_wait(act, qk_done, 2 * GROUPS * b)
                            nc.scalar.activation(ZH[:], turnp[:], ACT.Copy).then_inc(z_high, 1)

                        def v_copy(b, h):
                            act.wait_ge(v_done, b + 1)
                            some_wait(act, ctx_done, (b - 1) * GROUPS)
                            nc.scalar.activation(
                                V[:, h, :, :, 0:DK], mixp[:].rearrange("p (t a d) -> p t a d", t=TPB, d=DK),
                                ACT.Copy).then_inc(v_ready, 1)

                        def part(b, h, g, w, bank=mixp):
                            at = (b * GROUPS + g) * 2 + w
                            act.wait_ge(qk_done, at + 1)
                            some_wait(act, qk_ready, at)
                            if w == 0:
                                nc.scalar.activation(PART[:], bank[:], ACT.Identity,
                                                     scale=CT[:, CONST["pick_q"]]).then_inc(part_ready, 1)
                            else:
                                nc.scalar.activation(PART[:], bank[:], ACT.Identity, scale=CT[:, CONST["pick_k"]],
                                                     bias=CT[:, CONST["bias_k"]]).then_inc(part_ready, 1)

                        def unit_exp(s, g, k):
                            kb, j, m, w = KUNITS[k]
                            act.wait_ge(scoret_done, s * NU + k + 1)
                            if k == 0:
                                some_wait(act, ctx_done, s - 1)
                            nc.scalar.activation(PT[:, g % 2, j:j + m, KOFF[kb]:KOFF[kb] + w],
                                                 scoret[RINGT[g][k]][:, 0:m * w].rearrange("p (m w) -> p m w", m=m),
                                                 ACT.Exp, scale=SCALE).then_inc(exp_done, 1)

                        def ctx_copy(s):
                            act.wait_ge(ctx_done, s + 1)
                            some_wait(act, ctx_turned, s)
                            nc.scalar.activation(CTX[:], ctxp[:], ACT.Copy).then_inc(ctx_ready, 1)

                        def cn_copy(b):
                            act.wait_ge(cn_turned, b + 1)
                            some_wait(act, out_done, b)
                            nc.scalar.activation(CNT[:], turnp[:], ACT.Copy).then_inc(cnt_ready, 1)

                        def before():
                            z_copy(0)
                            v_copy(0, 0)
                            for g in range(GROUPS):
                                for w in range(2):
                                    part(0, 0, g, w, first_banks[(2 * g + w) % len(first_banks)])
                            z_copy(1)

                        def step(s, g, h, b):
                            next_batch = not known(s) or b + 1 < B
                            for k in range(NU):
                                unit_exp(s, g, k)
                                if k == 1 and (not known(s) or s > 0):
                                    ctx_copy(s - 1)
                                if k == 2 and g == 0 and next_batch:
                                    v_copy(b + 1, 1 - h)
                                if next_batch and (g, k) in PROJECT_AT:
                                    part(b + 1, 1 - h, *PROJECT_AT[g, k])
                                if k == 9 and g == 0 and (not known(b) or b > 0):
                                    cn_copy(b - 1)
                                if k == 10 and g == 3 and (not known(b) or b + 2 < B):
                                    z_copy(b + 2)

                        over_steps(act, step, before)
                        ctx_copy(STEPS - 1)
                        cn_copy(B - 1)

                    @block.gpsimd
                    def _(pool):
                        ln.finish(pool, nc.gpsimd, 0, 0)
                        nc.gpsimd.memset(KPAD[:].bitcast(F32), 0.0).then_inc(keys_zeroed, 1)
                        ln.finish(pool, nc.gpsimd, 1, 1)
                        for b in range(2, B):
                            pool.wait_ge(xn_ready, (b - 1) * TPB)
                            ln.finish(pool, nc.gpsimd, b, b % 2)

                    @block.tensor
                    def _(pe):
                        pe.wait_ge(weights_in, 80)
                        pe.wait_ge(w_ready, 1)

                        def turn_x(b):
                            pe.wait_ge(xn_ready, (b + 1) * TPB)
                            if known(b) and b < 2:
                                some_wait(pe, z_ready, b)
                            else:
                                pe.wait_ge(qm_ready, (b - 1) * GROUPS + 1)
                            for u in range(TPB):
                                last = nc.tensor.transpose(turnp[:, u * P:(u + 1) * P], XN[:, u, :], IDENT)
                            last.then_inc(turned, 1)

                        def values(b):
                            pe.wait_ge(z_ready, b + 1)
                            some_wait(pe, qk_ready, 2 * GROUPS * b)
                            for u in range(TPB):
                                for i, (z, w) in enumerate(((ZH, WH), (ZH, WL), (ZL, WH))):
                                    last = nc.tensor.matmul(mixp[:, u * P:(u + 1) * P], z[:, u * P:(u + 1) * P],
                                                            w[:, 2 * GROUPS, :], start=(i == 0), stop=(i == 2))
                            last.then_inc(v_done, 1)

                        def project(b, g, w, bank=mixp, banks=1):
                            if g == 0 and w == 0:
                                pe.wait_ge(v_ready, b + 1)
                            if g == 2 and w == 0:
                                some_wait(pe, x_done, b - 1)
                            some_wait(pe, qk_ready, (b * GROUPS + g) * 2 + w + 1 - banks)
                            for i, (weight, z) in enumerate(((WH, ZH), (WL, ZH), (WH, ZL))):
                                last = nc.tensor.matmul(bank[:], weight[:, w * GROUPS + g, :], z[:], start=(i == 0),
                                                        stop=(i == 2))
                            last.then_inc(qk_done, 1)

                        def unit_score(s, g, h, k):
                            qt, j, m, w = QUNITS[k]
                            bank = score[RING[g][k]]
                            some_wait(pe, max_done, s * NU + k + 1 - since(RING, g, k))
                            for a in range(m):
                                nc.tensor.matmul(bank[:, a * w:(a + 1) * w], Q[:, h, g, qt * P:(qt + 1) * P],
                                                 KPAD[:, h, g * GH + j + a, 0:w], start=True, stop=False)
                                last = nc.tensor.matmul(bank[:, (a + 1) * w - P:(a + 1) * w], MASK[:, 0, :],
                                                        MASK[:, 1, :], start=False, stop=True)
                            last.then_inc(score_done, 1)

                        def turn_max(s):
                            pe.wait_ge(spread_ready, s + 1)
                            some_wait(pe, cn_ready, s - 1)
                            for u in range(TPB):
                                last = nc.tensor.transpose(turnp[:, u * P:(u + 1) * P], SPREAD[:, u, :], IDENT)
                            last.then_inc(spread_turned, 1)

                        def unit_scoret(s, g, h, k):
                            kb, j, m, w = KUNITS[k]
                            bank = scoret[RINGT[g][k]]
                            some_wait(pe, exp_done, s * NU + k + 1 - since(RINGT, g, k))
                            for a in range(m):
                                nc.tensor.matmul(bank[:, a * w:(a + 1) * w], KPAD[:, h, g * GH + j + a, kb * P:(kb + 1) * P],
                                                 QM[:, g % 2, kb * P:S], start=True, stop=False)
                                last = nc.tensor.matmul(bank[:, a * w:a * w + P], MASK[:, 0, :], MASK[:, 2, :],
                                                        start=False, stop=True)
                            last.then_inc(scoret_done, 1)

                        def weigh(s, g, h, kb):
                            need = {0: 4, 1: 8, 2: 10, 3: 11}[kb]
                            pe.wait_ge(exp_done, s * NU + need)
                            if kb == 0:
                                some_wait(pe, ctx_ready, s)
                            for j in range(GH):
                                last = nc.tensor.matmul(ctxp[j * QR:(j + 1) * QR, kb * P:S], V[:, h, kb, g * GH + j, :],
                                                        PT[:, g % 2, j, KOFF[kb]:KOFF[kb] + S - kb * P],
                                                        start=(kb == 0), stop=(kb == TPB - 1),
                                                        tile_position=(0, j * QR))
                            if kb == TPB - 1:
                                last.then_inc(ctx_done, 1)

                        def turn_ctx(s, g, b):
                            pe.wait_ge(ctx_ready, s + 1)
                            if not known(s) or s + 1 < STEPS:
                                pe.wait_ge(qm_ready, s + 2)
                            else:
                                pe.wait_ge(cn_ready, s)
                            if g == GROUPS - 1:
                                pe.wait_ge(z_ready, b + 2 if not known(b) or b + 2 < B else B)
                            if g == 0:
                                some_wait(pe, cnt_ready, b)
                            for u in range(TPB):
                                last = nc.tensor.transpose(turnp[:, u * P:(u + 1) * P], CTX[:, u * P:(u + 1) * P], IDENT)
                            last.then_inc(ctx_turned, 1)

                        def turn_cn(b):
                            pe.wait_ge(cn_ready, (b + 1) * GROUPS)
                            if not known(b) or b + 1 < B:
                                pe.wait_ge(qm_ready, (b + 1) * GROUPS + 2)
                            for u in range(TPB):
                                last = nc.tensor.transpose(turnp[:, u * P:(u + 1) * P], CN[:, u, :], IDENT)
                            last.then_inc(cn_turned, 1)

                        def project_out(b):
                            pe.wait_ge(cnt_ready, b + 1)
                            some_wait(pe, x_done, b)
                            if known(b) and b + 2 >= B:
                                pe.wait_ge(qk_ready, 2 * GROUPS * B)
                            else:
                                pe.wait_ge(qk_ready, 2 * GROUPS * (b + 2) + 4)
                            for u in range(TPB):
                                last = nc.tensor.matmul(mixp[:, u * P:(u + 1) * P], CNT[:, u * P:(u + 1) * P], WO[:],
                                                        start=True, stop=True)
                            last.then_inc(out_done, 1)

                        def before():
                            turn_x(0)
                            values(0)
                            for g in range(GROUPS):
                                for w in range(2):
                                    project(0, g, w, first_banks[(2 * g + w) % len(first_banks)], len(first_banks))
                            turn_x(1)
                            pe.wait_ge(qk_ready, 2 * GROUPS)
                            pe.wait_ge(mask_ready, 1)
                            pe.wait_ge(zeros_set, 3)
                            for s in range(2):
                                pe.wait_ge(kpad_in[s], 16 * GH)
                                for k in range(NU):
                                    unit_score(s, s, 0, k)
                                if s == 0:
                                    pe.wait_ge(z_ready, 2)
                                    turn_max(0)

                        def step(s, g, h, b):
                            prev = not known(s) or s > 0
                            more = not known(s) or s + 2 < STEPS
                            next_batch = not known(s) or b + 1 < B
                            prev_batch = not known(b) or b > 0
                            hn = h if g < 2 else 1 - h
                            pe.wait_ge(qm_ready, s + 1)
                            if more:
                                pe.wait_ge(kpad_in[(g + 2) % GROUPS], 16 * GH * (b + (1 if g < 2 else 2)))
                            for k in range(NU):
                                unit_scoret(s, g, h, k)
                                if k == 0 and prev:
                                    hp = h if g > 0 else 1 - h
                                    weigh(s - 1, (g - 1) % GROUPS, hp, 2)
                                    weigh(s - 1, (g - 1) % GROUPS, hp, 3)
                                if k == 1 and g == 0 and next_batch:
                                    values(b + 1)
                                if next_batch and (g, k) in PROJECT_AT:
                                    project(b + 1, *PROJECT_AT[g, k])
                                if k == 3 and prev:
                                    turn_ctx(s - 1, (g - 1) % GROUPS, b if g > 0 else b - 1)
                                if k == 6 and (not known(s) or s + 1 < STEPS):
                                    turn_max(s + 1)
                                if k == 8:
                                    weigh(s, g, h, 0)
                                if k == 9 and g == 0 and prev_batch:
                                    turn_cn(b - 1)
                                if k == 9 and g == 1 and prev_batch:
                                    project_out(b - 1)
                                if k == 9 and g == 3 and (not known(b) or b + 2 < B):
                                    turn_x(b + 2)
                                if more:
                                    unit_score(s + 2, (g + 2) % GROUPS, hn, k)
                                if k == NU - 1:
                                    weigh(s, g, h, 1)

                        over_steps(pe, step, before)
                        weigh(STEPS - 1, GROUPS - 1, 1, 2)
                        weigh(STEPS - 1, GROUPS - 1, 1, 3)
                        turn_ctx(STEPS - 1, GROUPS - 1, B - 1)
                        turn_cn(B - 1)
                        project_out(B - 1)

        def new_semaphores():
            nc.clear_and_free_semaphores(nc.allocated_since(no_semaphores))
            nc.all_engine_barrier()

        def store():
            stored = sem("stored")
            with nc.Block() as block:
                @block.sync
                def _(sp):
                    sp.dma_start(out_tok, X[:]).then_inc(stored, 16)
                    sp.wait_ge(stored, 16)

        with ExitStack() as experts_ctx:
            W1, W3 = (sb(name, [P, E, FF], F32, experts_ctx) for name in ("W1", "W3"))
            W2 = sb("W2", [P, E, FC, D], F32, experts_ctx)
            W1H, W3H = (sb(name, [P, E, FF], F32R, experts_ctx) for name in ("W1H", "W3H"))
            GW = sb("GW", [P, E], F32, experts_ctx)
            experts(0)
            scan_layer("c0_")
            new_semaphores()
            experts(1)
        new_semaphores()
        shifted_ffn(0, "c1_")
        attention()
        shifted_ffn(1)
        store()


def lay_out(d):
    f = lambda a: np.ascontiguousarray(np.asarray(a))
    i = np.arange(P)
    vecs = np.zeros((P, 8 + KC), np.float32)
    for v, name in enumerate(("L0_attn_norm_scale", "L0_attn_conv_b", "L0_attn_dt_bias", "L1_ffn_mu_r", "L1_ffn_mu_k")):
        vecs[:, v] = f(d[name])
    conv_diag = np.zeros((P, KC, P), np.float32)
    for w in range(KC):
        conv_diag[i, w, i] = f(d["L0_attn_conv_w"])[:, 0, w]
    w = f(d["L0_attn_in_proj_w"])
    v = w[:, D:2 * D]
    swapped = v.reshape(D, HM, 2, DH // 2)[:, :, ::-1, :].reshape(D, D)
    in_proj = f(np.stack([w[:, 0:D], w[:, 2 * D:3 * D], v, swapped], 1))
    head_mix = np.zeros((P, P), np.float32)
    for r in range(DH):
        head_mix[np.ix_(np.arange(HM) * DH + r, np.arange(HM) * DH + r)] = f(d["L0_attn_head_mix"])
    ffn_w = f(np.stack([f(d["L1_ffn_W_r"]).T, f(d["L1_ffn_W_k"]).T, f(d["L1_ffn_W_v"]).T], 1))
    qkv = f(d["L1_attn_W_qkv"])
    qk = np.zeros((2, P, GROUPS, P), np.float32)
    for w in range(2):
        for h in range(HA):
            for part in range(3):
                at = QR * (h % GH) + DK * part
                qk[w, :, h // GH, at:at + DK] = qkv[w, h].T
    masks = np.zeros((P, 3, P), np.float32)
    masks[:, 0] = np.eye(P)
    masks[:, 1] = np.where(i[None, :] > i[:, None], NEG, 0)
    masks[:, 2] = np.where(i[:, None] > i[None, :], NEG, 0)
    return dict(x=f(d["L0_attn_x"]).reshape(T, D), consts=constant_table(), gate_w=f(d["L0_ffn_gate_w"]),
                w1=f(d["L0_ffn_w1"]), w3=f(d["L0_ffn_w3"]), w2=f(d["L0_ffn_w2"]), vecs=vecs, conv_diag=conv_diag,
                in_proj=in_proj, head_mix=head_mix, out_proj=f(d["L0_attn_out_proj_w"]), ffn_w=ffn_w,
                w_q=qk[0], w_k=qk[1], w_v=f(qkv[2].reshape(D, D).T), w_o=f(f(d["L1_attn_W_o"]).T), masks=masks)


def kernel(**inputs):
    import concourse.bacc as _bacc
    from concourse.bass_utils import run_bass_kernel_spmd as _run

    nc = _bacc.Bacc("TRN2", target_bir_lowering=False, num_devices=1)
    arrays, args = {}, {}
    for name, a in lay_out(inputs).items():
        arrays[f"in_{name}_dram"] = a
        args[name] = nc.dram_tensor(f"in_{name}_dram", a.shape, mybir.dt.from_np(a.dtype), kind="ExternalInput").ap()
    out = nc.dram_tensor("out_0_dram", (T, D), F32, kind="ExternalOutput").ap()
    build_macaron(nc, out=out, **args)
    r = _run(nc, [arrays], core_ids=[0])
    return r.results[0]["out_0_dram"].reshape(B, S, D)
```
